# Optimizing a Trainium2 kernel written in Bass

```python
import numpy as np
import jax
import jax.numpy as jnp

def _softmax(x, axis=-1):
    return jax.nn.softmax(x, axis=axis)

def _gelu(x):
    return jax.nn.gelu(x, approximate=True)

def _silu(x):
    return jax.nn.silu(x)

def _sigmoid(x):
    return jax.nn.sigmoid(x)

def _layernorm(x, axis=-1, eps=1e-05):
    m = jnp.mean(x, axis=axis, keepdims=True)
    v = jnp.var(x, axis=axis, keepdims=True)
    return (x - m) / jnp.sqrt(v + eps)

def _scatter_add(tgt, idx, src, axis=0):
    return tgt.at[idx].add(src)

def _segment_sum(src, seg, n):
    return jax.ops.segment_sum(src, seg, n)
kernel_name = 'mk_adj_preln_d2_adj_r2_3fe8db'

def setup_inputs(seed: int=0):
    np.random.seed(seed)
    _w = jnp.asarray

    def _rec_inputs():
        import jax
        import jax.numpy as jnp
        _gk = jax.random.key(seed)
        x = -0.0005207 + 1.001 * jax.random.normal(jax.random.fold_in(_gk, 1), (4096, 128), jnp.float32)
        _w = (1.0 + jnp.arange(4096, dtype=jnp.float32)) ** (-0.5)
        _w = _w / _w.mean()
        _pij = jnp.clip(0.000976562 * _w[:, None] * _w[None, :], 0.0, 1.0)
        _a = jax.random.uniform(jax.random.fold_in(_gk, 2), (4096, 4096)) < _pij
        _a = jnp.logical_or(_a, jnp.eye(4096, dtype=bool))
        _af = _a.astype(jnp.float32)
        _af = _af * jax.random.uniform(jax.random.fold_in(_gk, 3), (4096, 4096), jnp.float32, 0.05, 1)
        adj = _af
        return (x, adj)
    x, adj = _rec_inputs()

    def _L0_gnn_setup():
        import jax, jax.numpy as jnp
        import numpy as np
        N, DIM = (8192, 128)

        def _gru_cell(x, h, W_ih, W_hh, b_ih, b_hh):
            gi = x @ W_ih.T + b_ih
            gh = h @ W_hh.T + b_hh
            i_r, i_z, i_n = jnp.split(gi, 3, axis=-1)
            h_r, h_z, h_n = jnp.split(gh, 3, axis=-1)
            r = jax.nn.sigmoid(i_r + h_r)
            z = jax.nn.sigmoid(i_z + h_z)
            n = jnp.tanh(i_n + r * h_n)
            return (1.0 - z) * n + z * h
        key = jax.random.key(seed)
        ks = jax.random.split(key, 8)
        states = jax.random.normal(ks[0], (N, DIM), dtype=jnp.float32)
        adj = jax.random.uniform(ks[1], (N, N), dtype=jnp.float32)
        s = 1.0 / np.sqrt(DIM)
        W_msg = jax.random.uniform(ks[2], (DIM, DIM), minval=-s, maxval=s, dtype=jnp.float32)
        b_msg = jax.random.uniform(ks[3], (DIM,), minval=-s, maxval=s, dtype=jnp.float32)
        W_ih = jax.random.uniform(ks[4], (3 * DIM, DIM), minval=-s, maxval=s, dtype=jnp.float32)
        W_hh = jax.random.uniform(ks[5], (3 * DIM, DIM), minval=-s, maxval=s, dtype=jnp.float32)
        b_ih = jax.random.uniform(ks[6], (3 * DIM,), minval=-s, maxval=s, dtype=jnp.float32)
        b_hh = jax.random.uniform(ks[7], (3 * DIM,), minval=-s, maxval=s, dtype=jnp.float32)
        return {'states': states, 'adj': adj, 'W_msg': W_msg, 'b_msg': b_msg, 'W_ih': W_ih, 'W_hh': W_hh, 'b_ih': b_ih, 'b_hh': b_hh}
    _L0_gnn_all = _L0_gnn_setup()
    _L0_gnn_in = {k: v for k, v in _L0_gnn_all.items() if k in ('W_msg', 'b_msg', 'W_ih', 'W_hh', 'b_ih', 'b_hh')}
    del _L0_gnn_all

    def _L1_gnn_setup():
        import jax, jax.numpy as jnp
        import numpy as np
        N = 4096
        D = 128
        EPS = 1e-07
        NEG = -1000000000.0
        key = jax.random.key(seed)
        kx, ka, kb = jax.random.split(key, 3)
        x = jax.random.normal(kx, (N, D), dtype=jnp.float32)
        adj = jax.random.randint(ka, (N, N), 0, 2).astype(jnp.float32)
        adj = adj.at[jnp.arange(N), jnp.arange(N)].set(1.0)
        beta = jax.random.uniform(kb, (1,), dtype=jnp.float32)
        return {'x': x, 'adj': adj, 'beta': beta}
    _L1_gnn_all = _L1_gnn_setup()
    _L1_gnn_in = {k: v for k, v in _L1_gnn_all.items() if k in ('beta',)}
    del _L1_gnn_all
    return {'x': x, 'adj': adj, 'L0_gnn_W_msg': _L0_gnn_in['W_msg'], 'L0_gnn_b_msg': _L0_gnn_in['b_msg'], 'L0_gnn_W_ih': _L0_gnn_in['W_ih'], 'L0_gnn_W_hh': _L0_gnn_in['W_hh'], 'L0_gnn_b_ih': _L0_gnn_in['b_ih'], 'L0_gnn_b_hh': _L0_gnn_in['b_hh'], 'L1_gnn_beta': _L1_gnn_in['beta']}

def reference(x, adj, L0_gnn_W_msg, L0_gnn_b_msg, L0_gnn_W_ih, L0_gnn_W_hh, L0_gnn_b_ih, L0_gnn_b_hh, L1_gnn_beta):
    import jax
    import jax.numpy as jnp

    def _L0_gnn_ref(states, adj, W_msg, b_msg, W_ih, W_hh, b_ih, b_hh):
        import jax, jax.numpy as jnp
        import numpy as np
        N, DIM = (8192, 128)

        def _gru_cell(x, h, W_ih, W_hh, b_ih, b_hh):
            gi = x @ W_ih.T + b_ih
            gh = h @ W_hh.T + b_hh
            i_r, i_z, i_n = jnp.split(gi, 3, axis=-1)
            h_r, h_z, h_n = jnp.split(gh, 3, axis=-1)
            r = jax.nn.sigmoid(i_r + h_r)
            z = jax.nn.sigmoid(i_z + h_z)
            n = jnp.tanh(i_n + r * h_n)
            return (1.0 - z) * n + z * h
        agg = adj @ states
        msg = jax.nn.relu(agg @ W_msg.T + b_msg)
        return _gru_cell(msg, states, W_ih, W_hh, b_ih, b_hh)

    def _L1_gnn_ref(x, adj, beta):
        import jax, jax.numpy as jnp
        import numpy as np
        N = 4096
        D = 128
        EPS = 1e-07
        NEG = -1000000000.0
        norm2 = jnp.linalg.norm(x, axis=1, keepdims=True)
        cos = beta * (x @ x.T) / (norm2 @ norm2.T + EPS)
        masked = cos + (1.0 - adj) * NEG
        P = jax.nn.softmax(masked, axis=1)
        return P @ x
    h = jnp.maximum(_layernorm(x, axis=-1), 0.0)
    x = x + _L0_gnn_ref(h, adj, L0_gnn_W_msg, L0_gnn_b_msg, L0_gnn_W_ih, L0_gnn_W_hh, L0_gnn_b_ih, L0_gnn_b_hh)
    h = jnp.maximum(_layernorm(x, axis=-1), 0.0)
    x = x + _L1_gnn_ref(h, adj, L1_gnn_beta)
    return x

_drawn_inputs = setup_inputs


def setup_inputs(seed=0):
    import zlib

    import numpy as np

    out = dict(_drawn_inputs(seed))
    spreads = {}
    factors = {'L0_gnn_b_msg': 6.7, 'L0_gnn_b_ih': 2.681, 'L0_gnn_b_hh': 4.664}
    for name, (base, spread) in spreads.items():
        noise = np.random.default_rng([zlib.crc32(name.encode()), seed]).standard_normal(out[name].shape)
        drawn = base * np.exp(spread * noise) if base else spread * noise
        out[name] = jnp.asarray(drawn.astype(out[name].dtype))
    for name, factor in factors.items():
        out[name] = (out[name] * factor).astype(out[name].dtype)
    return out
```

```python
import concourse.bass as bass
from concourse import mybir
from contextlib import ExitStack


def gnn_gru_then_masked_attention(
    nc: bass.Bass,
    x: bass.AP,
    adj: bass.AP,
    W_msg: bass.AP,
    b_msg: bass.AP,
    W_ih: bass.AP,
    W_hh: bass.AP,
    b_ih: bass.AP,
    b_hh: bass.AP,
    beta: bass.AP,
    out: bass.AP,
):
    f32, f16, i32 = mybir.dt.float32, mybir.dt.float16, mybir.dt.int32
    ALU = mybir.AluOpType
    ACT = mybir.ActivationFunctionType
    AX = mybir.AxisListType

    N, D = x.shape
    P = 128
    NT = N // P
    R = 4
    CH = R * P
    NC = N // CH
    PIECE = 512
    NP = N // PIECE
    KB = PIECE // P
    NK = N // P
    SLOTS = 4
    NPAIR = NK // 2
    SPLIT = (2, 6, 10, 14)
    WHOLE = tuple(p for p in range(NPAIR) if p not in SPLIT)
    NSPLIT, NWHOLE = 2, 3
    AHEAD = 3
    NB = 4
    W = 2 * D + 1

    LN_EPS = 1e-5
    NEG = 1e9
    H_SCALE = 2.0 ** 8
    A_SCALE = 2.0 ** 10
    Q_SCALE = 2.0 ** 8
    L_SCALE = Q_SCALE * Q_SCALE
    P_LOG_SCALE = 6.931471805599453

    adj_v = adj.rearrange("(c r p) k -> p c r k", p=P, r=R)
    x_v = x.rearrange("(t p) d -> p t d", p=P)
    out_v = out.rearrange("(c r p) d -> p c r d", p=P, r=R)

    ctx = ExitStack()
    with ctx:
        def sb(name, shape, dt):
            return ctx.enter_context(nc.sbuf_tensor(name, shape, dt))

        def sem(name):
            return ctx.enter_context(nc.semaphore(name))

        ring = sb("adj_ring", [P, SLOTS, R, PIECE], f32)
        xs = sb("xs", [P, NT, D], f32)
        h0 = sb("h0", [P, NT, D], f32)
        h0_hi = sb("h0_hi", [P, NT, D], f16)
        h0_lo = sb("h0_lo", [P, NT, D], f16)
        whole = sb("whole", [P, NWHOLE, 2 * CH], f32)
        split_hi = sb("split_hi", [P, NSPLIT, 2 * CH], f16)
        split_lo = sb("split_lo", [P, NSPLIT, 2 * CH], f16)
        q_hi = sb("q_hi", [P, N], f16)
        q_lo = sb("q_lo", [P, N], f16)
        k_hi = sb("k_hi", [P, N], f16)
        k_lo = sb("k_lo", [P, N], f16)
        vals = sb("vals", [P, NT, W + 1], f16)
        w_nat = sb("w_nat", [P, 7, D], f32)
        wT = sb("wT", [P, 7, D], f32)
        ident = sb("ident", [P, P], f32)
        b_m = sb("b_m", [P, 1], f32)
        b_i = sb("b_i", [P, 3], f32)
        b_h = sb("b_h", [P, 3], f32)
        b_rz = sb("b_rz", [P, 2], f32)
        bt = sb("bt", [P, 1], f32)
        bt_neg = sb("bt_neg", [P, 1], f32)
        k_scale = sb("k_scale", [P, 1], f32)
        p_bias = sb("p_bias", [P, 1], f32)
        stats = sb("stats", [P, NT, 6], f32)
        mv = sb("mv", [P, NT, 2], f32)
        va = sb("va", [P, NT], f32)
        rs = sb("rs", [P, NT], f32)
        nt1 = sb("nt1", [P, NT], f32)
        nt2 = sb("nt2", [P, NT], f32)
        mx = sb("mx", [P, NP, NT], f32)
        m_row = sb("m_row", [P, NT], f32)
        h_st = sb("h_st", [P, R, D], f32)
        hT = sb("hT", [P, CH], f32)
        aggT = sb("aggT", [P, CH], f32)
        msgT = sb("msgT", [P, CH], f32)
        rT = sb("rT", [P, CH], f32)
        zT = sb("zT", [P, CH], f32)
        tT = sb("tT", [P, CH], f32)
        nT = sb("nT", [P, CH], f32)
        dT = sb("dT", [P, CH], f32)
        x1_st = sb("x1_st", [P, R, D], f32)
        h1 = sb("h1", [P, R, D], f32)
        h1n = sb("h1n", [P, R, D], f32)
        sq = sb("sq", [P, R, D], f32)
        n2 = sb("n2", [P, R], f32)
        n2c = sb("n2c", [P, R], f32)
        rn = sb("rn", [P, R], f32)
        c1 = sb("c1", [P, R], f32)
        c2 = sb("c2", [P, R], f32)
        p_hi = sb("p_hi", [P, NB, CH], f16)
        p_lo = sb("p_lo", [P, NB, CH], f16)
        o_den = sb("o_den", [P, R], f32)
        o_t = sb("o_t", [P, R, D], f32)
        o_st = sb("o_st", [P, R, D], f32)
        masks = h0[:, :, :].rearrange("p (s r q) d -> p s r (q d)", s=2, r=R)

        ps = ctx.enter_context(nc.psum_tensor("ps", [P, 8, 512], f32))
        tile2 = [ps[:, 2 * b:2 * b + 2, :].rearrange("p a n -> p (a n)") for b in range(2)]
        AGG, G5, G6, G7 = (ps[:, b, :] for b in (4, 5, 6, 7))
        accs = [ps[:, 4 + r, :] for r in range(R)]

        s_x = [sem(f"x_loaded{g}") for g in range(4)]
        s_w = sem("weights_loaded")
        s_b = sem("biases_loaded")
        s_ring = [sem(f"ring_loaded{s}") for s in range(SLOTS)]
        s_ident0 = sem("ident_zeroed")
        s_ident = sem("ident_ready")
        s_ones = sem("ones_ready")
        s_wps = sem("weights_transposed")
        s_wsb = sem("weights_ready")
        s_h0 = sem("h0_ready")
        s_h0hi = sem("h0_hi_ready")
        s_h0lo = sem("h0_lo_ready")
        s_bias = sem("small_constants_ready")
        dve_seq = sem("dve_seq")
        dve_gru = sem("dve_gru")
        dve_out = sem("dve_out")
        pool_seq = sem("pool_seq")
        s_t = sem("adj_transposed")
        s_hi = sem("adj_hi_ready")
        s_lo = sem("adj_lo_ready")
        s_agg = sem("pair_aggregated")
        s_mxd = sem("row_maxima_taken")
        s_aggT = sem("agg_evacuated")
        s_hst = sem("h_staged")
        s_hTps = sem("h_transposed")
        s_hT = sem("hT_ready")
        s_mps = sem("msg_product")
        s_msg = sem("msg_ready")
        s_rzps = sem("rz_products")
        s_rz = sem("rz_ready")
        s_nps = sem("n_products")
        s_tT = sem("n_argument_ready")
        s_nT = sem("n_ready")
        s_g = sem("gru_ready")
        s_gps = sem("gru_transposed")
        s_x1 = sem("x1_ready")
        s_h1 = sem("h1_ready")
        s_n2 = sem("norms_ready")
        s_h1n = sem("h1_normalised")
        s_qps = sem("q_transposed")
        s_qk = sem("qk_hi_ready")
        s_vh = sem("vals_hi_ready")
        s_qkl = sem("qk_lo_ready")
        s_vl = sem("vals_lo_ready")
        s_m = sem("row_max_ready")
        s_ma = sem("mask_taken")
        s_mk = sem("mask_ready")
        s_s = sem("logits_ready")
        s_p = sem("probs_ready")
        s_pl = sem("probs_lo_ready")
        s_pv = sem("probs_used")
        s_acc = sem("acc_evacuated")
        s_out = sem("out_stored")

        def buffer(p):
            group, n = (SPLIT, NSPLIT) if p in SPLIT else (WHOLE, NWHOLE)
            i = group.index(p)
            return i % n, int(i < n), group[(i - n) % len(group)]

        assert len(SPLIT) % NSPLIT == 0 and len(WHOLE) % NWHOLE == 0

        def wait_left_psum(engine, c, p):
            if p in SPLIT:
                engine.wait_ge(s_lo, len(SPLIT) * c + SPLIT.index(p) + 1)
            else:
                engine.wait_ge(s_hi, NPAIR * c + p + 1)

        block = ctx.enter_context(nc.Block())

        @block.sync
        def _(sp):
            for g in range(4):
                sp.dma_start(xs[:, 8 * g:8 * g + 8, :], x_v[:, 8 * g:8 * g + 8, :]).then_inc(s_x[g], 16)

            def load(c, pc, waits):
                for semaphore, value in waits:
                    sp.wait_ge(semaphore, value)
                sp.dma_start(ring[:, pc % SLOTS, :, :],
                             adj_v[:, c, :, pc * PIECE:(pc + 1) * PIECE]).then_inc(s_ring[pc % SLOTS], 16)

            def free0(c, pc):
                return [(s_mxd, NP * c + pc + 1)]

            def free1(c, pc):
                return [(s_ma, NP * c + pc + 1)]

            def before(c, pc, free):
                return free(c - 1, pc + NP - SLOTS) if pc < SLOTS else free(c, pc - SLOTS)

            for pc in range(NP):
                load(0, pc, before(0, pc, free0) if pc >= SLOTS else [])
            with sp.Fori(1, NC) as c:
                for pc in range(NP):
                    load(c, pc, before(c, pc, free0))
            for pc in range(NP):
                load(0, pc, before(0, pc, free1) if pc >= SLOTS else free0(NC - 1, pc + NP - SLOTS))
            def store(c):
                sp.wait_ge(s_acc, R * (c + 1))
                sp.dma_start(out_v[:, c, :, :], o_st[:, :, :]).then_inc(s_out, 16)

            with sp.Fori(1, NC) as c:
                for pc in range(NP):
                    if pc == 6:
                        store(c - 1)
                    load(c, pc, before(c, pc, free1))
            store(NC - 1)
            sp.wait_ge(s_out, 16 * NC)

        @block.gpsimd
        def _(pool):
            seq = [0]

            def link(ins):
                seq[0] += 1
                ins.then_inc(pool_seq, 1)
                pool.wait_ge(pool_seq, seq[0])

            nc.gpsimd.memset(ident[:, :], 0.0).then_inc(s_ident0, 1)
            pool.wait_ge(s_ident0, 1)
            nc.gpsimd.affine_select(out=ident[:, :], in_=ident[:, :], compare_op=ALU.not_equal, fill=1.0,
                                    base=0, pattern=[[-1, P]], channel_multiplier=1).then_inc(s_ident, 1)
            nc.gpsimd.memset(vals[:, :, 2 * D:2 * D + 1], H_SCALE).then_inc(s_ones, 1)

            def stage_h(g):
                pool.wait_ge(s_h0, 4)
                nc.gpsimd.tensor_copy(h_st[:, :, :], h0[:, bass.ds(g * R, R), :]).then_inc(s_hst, 1)

            def gate(g, base):
                pool.wait_ge(s_nT, g + 1)
                pool.wait_ge(s_rz, g + 1)
                nc.gpsimd.tensor_tensor(dT[:, :], hT[:, :], nT[:, :], ALU.subtract).then_inc(pool_seq, 1)
                pool.wait_ge(pool_seq, base + 1)
                nc.gpsimd.tensor_tensor(dT[:, :], dT[:, :], zT[:, :], ALU.mult).then_inc(pool_seq, 1)
                pool.wait_ge(pool_seq, base + 2)
                nc.gpsimd.tensor_tensor(dT[:, :], dT[:, :], nT[:, :], ALU.add).then_inc(s_g, 1)

            with pool.Fori(0, NC) as g:
                pool.wait_ge(s_hTps, g)
                stage_h(g)
                gate(g, 2 * g)

        @block.scalar
        def _(act):
            act.dma_start(w_nat[:, 0, :], W_msg).then_inc(s_w, 16)
            act.dma_start(w_nat[:, 1:4, :], W_ih.rearrange("(g e) d -> e g d", g=3)).then_inc(s_w, 16)
            act.dma_start(w_nat[:, 4:7, :], W_hh.rearrange("(g e) d -> e g d", g=3)).then_inc(s_w, 16)
            act.dma_start(b_m[:, :], b_msg.rearrange("(e a) -> e a", a=1)).then_inc(s_b, 16)
            act.dma_start(b_i[:, :], b_ih.rearrange("(g e) -> e g", g=3),
                          allow_slow_non_contiguous=True).then_inc(s_b, 16)
            act.dma_start(b_h[:, :], b_hh.rearrange("(g e) -> e g", g=3),
                          allow_slow_non_contiguous=True).then_inc(s_b, 16)
            act.dma_start(bt[:, :], beta.partition_broadcast(P)).then_inc(s_b, 16)
            act.wait_ge(s_wps, 1)
            nc.scalar.activation(wT[:, 0:4, :], ps[:, 6, :].rearrange("p (g n) -> p g n", g=4),
                                 ACT.Copy).then_inc(s_wsb, 1)
            nc.scalar.activation(wT[:, 4:7, :], ps[:, 7, 0:3 * P].rearrange("p (g n) -> p g n", g=3),
                                 ACT.Copy).then_inc(s_wsb, 1)
            for g in range(4):
                act.wait_ge(s_h0, g + 1)
                nc.scalar.activation(h0_hi[:, 8 * g:8 * g + 8, :], h0[:, 8 * g:8 * g + 8, :], ACT.Copy,
                                     scale=H_SCALE).then_inc(s_h0hi, 1)

            def hi(c, p):
                buf, back, before = buffer(p)
                act.wait_ge(s_t, NPAIR * c + p + 1)
                if not (isinstance(c, int) and c < back):
                    act.wait_ge(s_agg, NPAIR * (c - back) + before + 1)
                if p in SPLIT:
                    nc.scalar.activation(split_hi[:, buf, :], tile2[p % 2], ACT.Copy,
                                         scale=A_SCALE).then_inc(s_hi, 1)
                else:
                    nc.scalar.activation(whole[:, buf, :], tile2[p % 2], ACT.Copy,
                                         scale=A_SCALE * H_SCALE).then_inc(s_hi, 1)

            def gru(g, p):
                if p == -1:
                    act.wait_ge(s_agg, NPAIR * (g + 1))
                    nc.scalar.activation(aggT[:, :], AGG, ACT.Copy, scale=1.0 / (H_SCALE * A_SCALE)).then_inc(s_aggT, 1)
                if p == 1:
                    act.wait_ge(s_hTps, g + 1)
                    nc.scalar.activation(hT[:, :], G5, ACT.Copy).then_inc(s_hT, 1)
                if p == 2:
                    act.wait_ge(s_mps, g + 1)
                    nc.scalar.activation(msgT[:, :], G6, ACT.Relu, bias=b_m[:, :]).then_inc(s_msg, 1)
                if p == 4:
                    act.wait_ge(s_rzps, g + 1)
                    nc.scalar.activation(rT[:, :], G7, ACT.Sigmoid, bias=b_rz[:, 0:1])
                    nc.scalar.activation(zT[:, :], G5, ACT.Sigmoid, bias=b_rz[:, 1:2]).then_inc(s_rz, 1)
                if p == 7:
                    act.wait_ge(s_tT, g + 1)
                    nc.scalar.activation(nT[:, :], tT[:, :], ACT.Tanh, bias=b_i[:, 2:3]).then_inc(s_nT, 1)
                if p == 12:
                    act.wait_ge(s_h1, g + 1)
                    for r in range(R):
                        last = nc.scalar.activation(sq[:, r, :], h1[:, r, :], ACT.Square, accum_out=n2[:, r:r + 1])
                    last.then_inc(s_n2, 1)
                    nc.scalar.activation(vals[:, bass.ds(g * R, R), D:2 * D], h1[:, :, :], ACT.Copy,
                                         scale=H_SCALE).then_inc(s_vh, 1)
                if p == 14:
                    act.wait_ge(s_qps, g + 1)
                    nc.scalar.activation(q_hi[:, bass.ds(g * CH, CH)], G6, ACT.Copy, scale=Q_SCALE)
                    nc.scalar.activation(k_hi[:, bass.ds(g * CH, CH)], G6, ACT.Copy,
                                         scale=k_scale[:, :]).then_inc(s_qk, 1)

            act.wait_ge(s_bias, 1)
            for p in range(NPAIR):
                hi(0, p)
            with act.Fori(1, NC) as c:
                gru(c - 1, -1)
                for p in range(NPAIR):
                    hi(c, p)
                    gru(c - 1, p)
            for p in range(-1, NPAIR):
                gru(NC - 1, p)

            def probs(c, n):
                U = NK * c + n
                act.wait_ge(s_s, U + 1)
                if not (isinstance(c, int) and U < NB):
                    act.wait_ge(s_pv, U - NB + 1)
                nc.scalar.activation(p_hi[:, n % NB, :], ps[:, n % NB, :], ACT.Exp,
                                     bias=p_bias[:, :], scale=1.0 / L_SCALE)
                nc.scalar.activation(ps[:, n % NB, :], ps[:, n % NB, :], ACT.Exp,
                                     bias=p_bias[:, :], scale=1.0 / L_SCALE).then_inc(s_p, 1)

            for n in range(NK):
                probs(0, n)
            with act.Fori(1, NC) as c:
                for n in range(NK):
                    probs(c, n)

        @block.vector
        def _(dve):
            seq = [0]

            def link(ins):
                seq[0] += 1
                ins.then_inc(dve_seq, 1)
                dve.wait_ge(dve_seq, seq[0])

            def rsqrt(y, a, t, h, chain):
                chain(nc.vector.tensor_scalar(y.bitcast(i32), a.bitcast(i32), -0.5, float(0x5F3759DF), ALU.mult, ALU.add))
                chain(nc.vector.tensor_scalar(h, a, -0.5, None, ALU.mult))
                for _ in range(3):
                    chain(nc.vector.tensor_tensor(t, y, y, ALU.mult))
                    chain(nc.vector.tensor_tensor(t, t, h, ALU.mult))
                    chain(nc.vector.scalar_tensor_tensor(out=y, in0=t, scalar=1.5, in1=y, op0=ALU.add, op1=ALU.mult))

            for g in range(4):
                dve.wait_ge(s_x[g], 16)
                for t in range(8 * g, 8 * g + 8):
                    last = nc.vector.bn_stats(stats[:, t, :], xs[:, t, :])
                link(last)
                for t in range(8 * g, 8 * g + 8):
                    last = nc.vector.bn_aggr(mv[:, t, :], stats[:, t, :])
                link(last)
                s8 = slice(8 * g, 8 * g + 8)
                link(nc.vector.tensor_scalar(va[:, s8], mv[:, s8, 1], LN_EPS, None, ALU.add))
                rsqrt(rs[:, s8], va[:, s8], nt1[:, s8], nt2[:, s8], link)
                for t in range(8 * g, 8 * g + 8):
                    last = nc.vector.tensor_scalar(h0[:, t, :], xs[:, t, :], mv[:, t, 0:1], rs[:, t:t + 1],
                                                   ALU.subtract, ALU.mult)
                link(last)
                nc.vector.tensor_scalar(h0[:, s8, :], h0[:, s8, :], 0.0, None, ALU.max).then_inc(s_h0, 1)
                dve.wait_ge(s_h0hi, g + 1)
                nc.vector.scalar_tensor_tensor(out=h0_lo[:, s8, :], in0=h0[:, s8, :], scalar=H_SCALE,
                                               in1=h0_hi[:, s8, :], op0=ALU.mult, op1=ALU.subtract).then_inc(s_h0lo, 1)
            dve.wait_ge(s_b, 64)
            nc.vector.tensor_tensor(b_rz[:, :], b_i[:, 0:2], b_h[:, 0:2], ALU.add)
            nc.vector.tensor_scalar(k_scale[:, :], bt[:, :], Q_SCALE, None, ALU.mult)
            link(nc.vector.tensor_scalar(bt_neg[:, :], bt[:, :], -1.0, None, ALU.mult))
            link(nc.vector.tensor_tensor(p_bias[:, :], bt[:, :], bt_neg[:, :], ALU.max))
            nc.vector.tensor_scalar(p_bias[:, :], p_bias[:, :], -1.0, P_LOG_SCALE, ALU.mult, ALU.add).then_inc(s_bias, 1)

            def lo(c, p):
                if p not in SPLIT:
                    return
                buf = buffer(p)[0]
                dve.wait_ge(s_hi, NPAIR * c + p + 1)
                nc.vector.scalar_tensor_tensor(out=split_lo[:, buf, :], in0=tile2[p % 2], scalar=A_SCALE,
                                               in1=split_hi[:, buf, :], op0=ALU.mult,
                                               op1=ALU.subtract).then_inc(s_lo, 1)

            def row_max(c, p):
                pc = p // 2
                if p % 2 == 1:
                    dve.wait_ge(s_t, NPAIR * c + p + 1)
                    dve.wait_ge(s_ring[pc % SLOTS], 16 * (2 * c + 1 + pc // SLOTS))
                    nc.vector.tensor_reduce(mx[:, pc, bass.ds(c * R, R)], ring[:, pc % SLOTS, :, :], AX.X,
                                            ALU.max).then_inc(s_mxd, 1)

            LINKS = 28

            def gru(g, p, done):
                def link_g(ins):
                    done[0] += 1
                    ins.then_inc(dve_gru, 1)
                    dve.wait_ge(dve_gru, LINKS * g + done[0])

                if p == 6:
                    dve.wait_ge(s_nps, g + 1)
                    link_g(nc.vector.scalar_tensor_tensor(out=tT[:, :], in0=G6, scalar=b_h[:, 2:3], in1=rT[:, :],
                                                          op0=ALU.add, op1=ALU.mult))
                    nc.vector.tensor_tensor(tT[:, :], G7, tT[:, :], ALU.add).then_inc(s_tT, 1)
                if p == 11:
                    x1 = xs[:, bass.ds(g * R, R), :]
                    dve.wait_ge(s_gps, g + 1)
                    nc.vector.tensor_tensor(x1_st[:, :, :], G5.rearrange("p (r d) -> p r d", r=R), x1,
                                            ALU.add).then_inc(s_x1, 1)
                    dve.wait_ge(s_x1, g + 1)
                    nc.vector.tensor_scalar(xs[:, bass.ds(g * R, 2), :], x1_st[:, 0:2, :], 1.0, None, ALU.mult)
                    for r in range(R):
                        last = nc.vector.bn_stats(stats[:, r, :], x1_st[:, r, :])
                    link_g(last)
                    nc.vector.tensor_scalar(xs[:, bass.ds(g * R + 2, 2), :], x1_st[:, 2:4, :], 1.0, None, ALU.mult)
                    for r in range(R):
                        last = nc.vector.bn_aggr(mv[:, r, :], stats[:, r, :])
                    link_g(last)
                    link_g(nc.vector.tensor_scalar(va[:, 0:R], mv[:, 0:R, 1], LN_EPS, None, ALU.add))
                    rsqrt(rs[:, 0:R], va[:, 0:R], nt1[:, 0:R], nt2[:, 0:R], link_g)
                    for r in range(R):
                        last = nc.vector.tensor_scalar(h1[:, r, :], x1_st[:, r, :],
                                                       mv[:, r, 0:1], rs[:, r:r + 1], ALU.subtract, ALU.mult)
                    link_g(last)
                    nc.vector.tensor_scalar(h1[:, :, :], h1[:, :, :], 0.0, None, ALU.max).then_inc(s_h1, 1)
                if p == 13:
                    dve.wait_ge(s_n2, g + 1)
                    link_g(nc.vector.tensor_scalar(n2c[:, :], n2[:, :], 1e-30, None, ALU.max))
                    rsqrt(rn[:, :], n2c[:, :], c1[:, :], c2[:, :], link_g)
                    for r in range(R):
                        last = nc.vector.tensor_scalar(h1n[:, r, :], h1[:, r, :], rn[:, r:r + 1], None, ALU.mult)
                    last.then_inc(s_h1n, 1)
                    dve.wait_ge(s_vh, g + 1)
                    nc.vector.scalar_tensor_tensor(out=vals[:, bass.ds(g * R, R), 0:D], in0=h1[:, :, :], scalar=H_SCALE,
                                                   in1=vals[:, bass.ds(g * R, R), D:2 * D], op0=ALU.mult,
                                                   op1=ALU.subtract).then_inc(s_vl, 1)
                if p == 15:
                    dve.wait_ge(s_qk, g + 1)
                    cols = bass.ds(g * CH, CH)
                    nc.vector.scalar_tensor_tensor(out=q_lo[:, cols], in0=G6, scalar=Q_SCALE, in1=q_hi[:, cols],
                                                   op0=ALU.mult, op1=ALU.subtract)
                    nc.vector.scalar_tensor_tensor(out=k_lo[:, cols], in0=G6, scalar=k_scale[:, :], in1=k_hi[:, cols],
                                                   op0=ALU.mult, op1=ALU.subtract).then_inc(s_qkl, 1)

            for p in range(NPAIR):
                lo(0, p)
                row_max(0, p)
            with dve.Fori(1, NC) as c:
                done = [0]
                for p in range(NPAIR):
                    lo(c, p)
                    gru(c - 1, p, done)
                    row_max(c, p)
                assert done[0] == LINKS, done
            dve.wait_ge(s_mxd, NP * NC)
            link(nc.vector.tensor_reduce(m_row[:, :], mx[:, :, :].rearrange("p h t -> p t h"), AX.X, ALU.max))
            link(nc.vector.tensor_scalar(m_row[:, :], m_row[:, :], -1.0, NEG * L_SCALE, ALU.add, ALU.mult))
            done = [0]
            for p in range(NPAIR):
                gru(NC - 1, p, done)

            def mask(c, pc, part):
                buf = pc % 2
                if part == 0:
                    dve.wait_ge(s_ring[pc % SLOTS], 16 * (2 * NC + 2 * c + 1 + pc // SLOTS))
                    nc.vector.tensor_scalar(masks[:, buf, :, :], ring[:, pc % SLOTS, :, :], -1.0, NEG * L_SCALE,
                                            ALU.add, ALU.mult).then_inc(s_ma, 1)
                    dve.wait_ge(s_ma, NP * c + pc + 1)
                else:
                    for r in (2 * part - 2, 2 * part - 1):
                        last = nc.vector.tensor_scalar(masks[:, buf, r, :], masks[:, buf, r, :],
                                                       m_row[:, bass.ds(c * R + r, 1)], None, ALU.subtract)
                    if part == 2:
                        last.then_inc(s_mk, 1)

            def probs_lo(c, n):
                dve.wait_ge(s_p, NK * c + n + 1)
                nc.vector.tensor_tensor(p_lo[:, n % NB, :], ps[:, n % NB, :], p_hi[:, n % NB, :],
                                        ALU.subtract).then_inc(s_pl, 1)

            def output(c, first):
                dve.wait_ge(s_pv, NK * (c + 1))
                for r in range(R):
                    nc.vector.reciprocal(o_den[:, r:r + 1], accs[r][:, 2 * D:2 * D + 1]).then_inc(dve_out, 1)
                    dve.wait_ge(dve_out, 2 * R * c + 2 * r + 1)
                    nc.vector.scalar_tensor_tensor(out=o_t[:, r, :], in0=accs[r][:, 0:D], scalar=o_den[:, r:r + 1],
                                                   in1=xs[:, bass.ds(c * R + r, 1), :].rearrange("p a d -> p (a d)"),
                                                   op0=ALU.mult, op1=ALU.add).then_inc(dve_out, 1)
                    dve.wait_ge(dve_out, 2 * R * c + 2 * r + 2)
                    if r == 0 and not first:
                        dve.wait_ge(s_out, 16 * c)
                    nc.vector.scalar_tensor_tensor(out=o_st[:, r, :], in0=accs[r][:, D:2 * D], scalar=o_den[:, r:r + 1],
                                                   in1=o_t[:, r, :], op0=ALU.mult, op1=ALU.add).then_inc(s_acc, 1)

            def chunk(c, first, final):
                for n in range(1, NK + 1):
                    if n < NK:
                        probs_lo(c, n)
                    elif not final:
                        probs_lo(c + 1, 0)
                    m, q = (n - 1) // KB, (n - 1) % KB
                    if q == 0:
                        dve.wait_ge(s_s, NK * c + KB * (m + 1))
                    if q < 3:
                        if m + 2 < NP:
                            mask(c, m + 2, q)
                        elif not final:
                            mask(c + 1, m + 2 - NP, q)
                output(c, first)

            for pc in range(2):
                for part in range(3):
                    mask(0, pc, part)
            probs_lo(0, 0)
            chunk(0, True, False)
            with dve.Fori(1, NC - 1) as c:
                chunk(c, False, False)
            chunk(NC - 1, False, True)

        @block.tensor
        def _(pe):
            def block_T(dst, src, first=True):
                return nc.tensor.matmul(dst, lhsT=src, rhs=ident[:, :], start=first, stop=True,
                                        is_transpose=True, skip_group_check=True)

            pe.wait_ge(s_w, 48)
            pe.wait_ge(s_ident, 1)
            for i in range(7):
                last = block_T(ps[:, 6 + i // 4, (i % 4) * P:(i % 4 + 1) * P], w_nat[:, i, :])
            last.then_inc(s_wps, 1)

            def transposes(c, p):
                pc, slot = p // 2, (p // 2) % SLOTS
                if p % 2 == 0:
                    pe.wait_ge(s_ring[slot], 16 * (2 * c + 1 + pc // SLOTS))
                if not (isinstance(c, int) and c == 0 and p < 2):
                    wait_left_psum(pe, c if p >= 2 else c - 1, (p - 2) % NPAIR)
                for b in range(2):
                    col = (2 * (p % 2) + b) * P
                    for r in range(R):
                        last = block_T(tile2[p % 2][:, b * CH + r * P:b * CH + (r + 1) * P],
                                       ring[:, slot, r, col:col + P])
                last.then_inc(s_t, 1)

            def aggregate(c, p):
                if isinstance(c, int) and c == 0 and p % 4 == 0:
                    pe.wait_ge(s_h0lo, p // 4 + 1)
                wait_left_psum(pe, c, p)
                if p == 0:
                    pe.wait_ge(s_aggT, c)
                buf = buffer(p)[0]
                for b in range(2):
                    k, cols = 2 * p + b, slice(b * CH, (b + 1) * CH)
                    first, final = k == 0, k == NK - 1
                    if p in SPLIT:
                        ah, al = split_hi[:, buf, cols], split_lo[:, buf, cols]
                        nc.tensor.matmul(AGG, lhsT=h0_hi[:, k, :], rhs=ah, start=first, stop=False)
                        nc.tensor.matmul(AGG, lhsT=h0_hi[:, k, :], rhs=al, start=False, stop=False)
                        last = nc.tensor.matmul(AGG, lhsT=h0_lo[:, k, :], rhs=ah, start=False, stop=final)
                    else:
                        last = nc.tensor.matmul(AGG, lhsT=h0[:, k, :], rhs=whole[:, buf, cols], start=first, stop=final)
                last.then_inc(s_agg, 1)

            def gru(g, p):
                if p == 0:
                    pe.wait_ge(s_hst, g + 1)
                    pe.wait_ge(s_x1, g)
                    for r in range(R):
                        last = block_T(G5[:, r * P:(r + 1) * P], h_st[:, r, :])
                    last.then_inc(s_hTps, 1)
                if p == 1:
                    pe.wait_ge(s_aggT, g + 1)
                    pe.wait_ge(s_qkl, g)
                    nc.tensor.matmul(G6, lhsT=wT[:, 0, :], rhs=aggT[:, :], start=True, stop=True).then_inc(s_mps, 1)
                if p == 3:
                    pe.wait_ge(s_msg, g + 1)
                    pe.wait_ge(s_hT, g + 1)
                    pe.wait_ge(s_tT, g)
                    for gate, dst in ((0, G7), (1, G5)):
                        nc.tensor.matmul(dst, lhsT=wT[:, 1 + gate, :], rhs=msgT[:, :], start=True, stop=False)
                        last = nc.tensor.matmul(dst, lhsT=wT[:, 4 + gate, :], rhs=hT[:, :], start=False, stop=True)
                    last.then_inc(s_rzps, 1)
                if p == 5:
                    pe.wait_ge(s_rz, g + 1)
                    nc.tensor.matmul(G6, lhsT=wT[:, 6, :], rhs=hT[:, :], start=True, stop=True)
                    nc.tensor.matmul(G7, lhsT=wT[:, 3, :], rhs=msgT[:, :], start=True, stop=True).then_inc(s_nps, 1)
                if p == 10:
                    pe.wait_ge(s_g, g + 1)
                    for r in range(R):
                        last = block_T(G5[:, r * P:(r + 1) * P], dT[:, r * P:(r + 1) * P])
                    last.then_inc(s_gps, 1)
                if p == 14:
                    pe.wait_ge(s_h1n, g + 1)
                    for r in range(R):
                        last = block_T(G6[:, r * P:(r + 1) * P], h1n[:, r, :])
                    last.then_inc(s_qps, 1)

            pe.wait_ge(s_wsb, 2)
            transposes(0, 0)
            transposes(0, 1)
            for p in range(NPAIR):
                if p + 2 < NPAIR:
                    transposes(0, p + 2)
                else:
                    transposes(1, p + 2 - NPAIR)
                aggregate(0, p)

            def chunk0(c, final):
                for p in range(NPAIR):
                    if p + 2 < NPAIR:
                        transposes(c, p + 2)
                    elif not final:
                        transposes(c + 1, p + 2 - NPAIR)
                    aggregate(c, p)
                    gru(c - 1, p)

            with pe.Fori(1, NC - 1) as c:
                chunk0(c, False)
            chunk0(NC - 1, True)
            for p in range(NPAIR):
                gru(NC - 1, p)

            def logits(c, n):
                pc, j = n // KB, n % KB
                U = NK * c + n
                if j == 0:
                    pe.wait_ge(s_mk, NP * c + pc + 1)
                if not (isinstance(c, int) and U < NB):
                    pe.wait_ge(s_pl, U - NB + 1)
                bank = ps[:, n % NB, :]
                for r in range(R):
                    block_T(bank[:, r * P:(r + 1) * P], masks[:, pc % 2, r, j * P:(j + 1) * P], first=(r == 0))
                kc = slice(n * P, (n + 1) * P)
                qc = bass.ds(c * CH, CH)
                for kk, qq in ((k_hi, q_hi), (k_hi, q_lo), (k_lo, q_hi)):
                    last = nc.tensor.matmul(bank, lhsT=kk[:, kc], rhs=qq[:, qc], start=False, stop=(kk is k_lo),
                                            skip_group_check=True)
                last.then_inc(s_s, 1)

            def weigh(c, n):
                pe.wait_ge(s_pl, NK * c + n + 1)
                for r in range(R):
                    if n == 0:
                        pe.wait_ge(s_acc, R * (c - 1) + r + 1) if not (isinstance(c, int) and c == 0) else None
                    rows = slice(r * P, (r + 1) * P)
                    hi = (p_hi[:, n % NB, rows], 0)
                    lo = (p_lo[:, n % NB, rows], D)
                    for i, (weights, col) in enumerate((hi, lo) if n == 0 else (lo, hi)):
                        last = nc.tensor.matmul(accs[r][:, col:W], lhsT=weights, rhs=vals[:, n, col:W],
                                                start=(n == 0 and i == 0), stop=(n == NK - 1 and i == 1),
                                                skip_group_check=True)
                last.then_inc(s_pv, 1)

            def chunk1(c, final):
                for n in range(NK):
                    if n + AHEAD < NK:
                        logits(c, n + AHEAD)
                    elif not final:
                        logits(c + 1, n + AHEAD - NK)
                    weigh(c, n)

            pe.wait_ge(s_qkl, NC)
            pe.wait_ge(s_vl, NC)
            pe.wait_ge(s_ones, 1)
            for n in range(AHEAD):
                logits(0, n)
            chunk1(0, False)
            with pe.Fori(1, NC - 1) as c:
                chunk1(c, False)
            chunk1(NC - 1, True)


_INS = ["x", "adj", "L0_gnn_W_msg", "L0_gnn_b_msg", "L0_gnn_W_ih", "L0_gnn_W_hh", "L0_gnn_b_ih", "L0_gnn_b_hh",
        "L1_gnn_beta"]
_OUTS = [((4096, 128), "float32")]


def kernel(**inputs):
    import numpy as _np
    import concourse.bacc as _bacc
    from concourse import mybir as _mybir
    from concourse.bass_utils import run_bass_kernel_spmd as _run

    nc = _bacc.Bacc("TRN2", target_bir_lowering=False, num_devices=1)
    arrays, args = {}, []
    for name in _INS:
        a = _np.ascontiguousarray(inputs[name])
        arrays[f"in_{name}_dram"] = a
        args.append(nc.dram_tensor(f"in_{name}_dram", a.shape, _mybir.dt.from_np(a.dtype), kind="ExternalInput").ap())
    for i, (shape, dtype) in enumerate(_OUTS):
        dt = _mybir.dt.from_np(_np.dtype(dtype))
        args.append(nc.dram_tensor(f"out_{i}_dram", shape, dt, kind="ExternalOutput").ap())
    gnn_gru_then_masked_attention(nc, *args)
    r = _run(nc, [arrays], core_ids=[0])
    return r.results[0]["out_0_dram"]
```

```python
import concourse.bass as bass
from concourse import mybir
from contextlib import ExitStack


def gnn_gru_then_masked_attention(
    nc: bass.Bass,
    x: bass.AP,
    adj: bass.AP,
    W_msg: bass.AP,
    b_msg: bass.AP,
    W_ih: bass.AP,
    W_hh: bass.AP,
    b_ih: bass.AP,
    b_hh: bass.AP,
    beta: bass.AP,
    out: bass.AP,
):
    f32, f16, i32 = mybir.dt.float32, mybir.dt.float16, mybir.dt.int32
    ALU = mybir.AluOpType
    ACT = mybir.ActivationFunctionType
    AX = mybir.AxisListType

    N, D = x.shape
    P = 128
    QD = 32
    G = 16
    NT = N // P
    R = 4
    CH = R * P
    NC = N // CH
    PIECE = 512
    NP = N // PIECE
    KB = PIECE // P
    NK = N // P
    SLOTS = 4
    NPAIR = NK // 2
    NGRP = 4
    NWHOLE, NTURN, NSPLIT = 2, 2, 4
    AHEAD = 3
    NB = 4
    W = 2 * D + 1

    LN_EPS = 1e-5
    NEG = 1e9
    H_SCALE = 2.0 ** 8
    A_SCALE = 2.0 ** 10
    Q_SCALE = 2.0 ** 8
    L_SCALE = Q_SCALE * Q_SCALE
    P_LOG_SCALE = 6.931471805599453

    adj_v = adj.rearrange("(c r p) k -> p c r k", p=P, r=R)
    adj_q = adj.rearrange("(c g r) (b a m) -> c b a r g m", r=QD, g=G, a=4, m=P)
    x_v = x.rearrange("(b p j) d -> p b (j d)", p=P, j=R)
    out_v = out.rearrange("(b p j) d -> p b j d", p=P, j=R)

    def tile_cols(ap, j):
        return ap.rearrange("p (i j) -> p j i", j=R)[:, j, :]

    ctx = ExitStack()
    with ctx:
        def sb(name, shape, dt):
            return ctx.enter_context(nc.sbuf_tensor(name, shape, dt))

        def sem(name):
            return ctx.enter_context(nc.semaphore(name))

        ring = sb("adj_ring", [P, SLOTS, R, PIECE], f32)
        xs = sb("xs", [P, NT, D], f32)
        h0 = sb("h0", [P, NT, D], f32)
        h0_hi = sb("h0_hi", [P, NT // 2, D], f16)
        h0_lo = sb("h0_lo", [P, NT // 2, D], f16)
        whole = sb("whole", [P, NWHOLE, 2 * CH], f32)
        turned = sb("turned", [P, NTURN, 2, CH], f32)
        split_hi = sb("split_hi", [P, NSPLIT, 2 * CH], f16)
        split_lo = sb("split_lo", [P, NSPLIT, 2 * CH], f16)
        q_hi = sb("q_hi", [P, N], f16)
        q_lo = sb("q_lo", [P, N], f16)
        k_hi = sb("k_hi", [P, N], f16)
        k_lo = sb("k_lo", [P, N], f16)
        vals = sb("vals", [P, NT, W + 1], f16)
        w_nat = sb("w_nat", [P, 7, D], f32)
        wT = sb("wT", [P, 7, D], f32)
        ident = sb("ident", [P, P], f32)
        b_m = sb("b_m", [P, 1], f32)
        b_i = sb("b_i", [P, 3], f32)
        b_h = sb("b_h", [P, 3], f32)
        b_rz = sb("b_rz", [P, 2], f32)
        bt = sb("bt", [P, 1], f32)
        bt_neg = sb("bt_neg", [P, 1], f32)
        k_scale = sb("k_scale", [P, 1], f32)
        p_bias = sb("p_bias", [P, 1], f32)
        stats = sb("stats", [P, NT, 6], f32)
        mv = sb("mv", [P, NT, 2], f32)
        va = sb("va", [P, NT], f32)
        rs = sb("rs", [P, NT], f32)
        nt1 = sb("nt1", [P, NT], f32)
        nt2 = sb("nt2", [P, NT], f32)
        mx = sb("mx", [P, NP, NC, R], f32)
        mxq = sb("mxq", [P, NP // 2, NC * G], f32)
        m_row = sb("m_row", [P, NT], f32)
        h_st = sb("h_st", [P, R, D], f32)
        hT = sb("hT", [P, CH], f32)
        aggT = sb("aggT", [P, CH], f32)
        msgT = sb("msgT", [P, CH], f32)
        rT = sb("rT", [P, CH], f32)
        zT = sb("zT", [P, CH], f32)
        tT = sb("tT", [P, CH], f32)
        nT = sb("nT", [P, CH], f32)
        dT = sb("dT", [P, CH], f32)
        x1_st = sb("x1_st", [P, R, D], f32)
        z1 = sb("z1", [P, R, D], f32)
        h1s = sb("h1s", [P, R, D], f32)
        h1n = sb("h1n", [P, R, D], f32)
        neg_mean = sb("neg_mean", [P, NT], f32)
        h_scale = sb("h_scale", [P, R], f32)
        mxo = sb("mxo", [P, NC * G], f32)
        sq = sb("sq", [P, R, D], f32)
        n2 = sb("n2", [P, R], f32)
        va2 = sb("va2", [P, 2 * R], f32)
        rs2 = sb("rs2", [P, 2 * R], f32)
        c1 = sb("c1", [P, 2 * R], f32)
        c2 = sb("c2", [P, 2 * R], f32)
        p_hi = sb("p_hi", [P, NB, CH], f16)
        p_lo = sb("p_lo", [P, NB, CH], f16)
        o_den = sb("o_den", [P, R], f32)
        o_t = sb("o_t", [P, R, D], f32)
        o_st = sb("o_st", [P, R, D], f32)
        masks = h0[:, :, :].rearrange("p (s r q) d -> p s r (q d)", s=2, r=R)

        ring_q = [ring[:, s, :, :].rearrange("p r n -> p (r n)").rearrange("p (g m) -> p g m", g=G)
                  for s in range(SLOTS)]
        ps = ctx.enter_context(nc.psum_tensor("ps", [P, 8, 512], f32))
        tile2 = [ps[:, 2 * b:2 * b + 2, :].rearrange("p a n -> p (a n)") for b in range(2)]
        AGG, G5, G6, G7 = (ps[:, b, :] for b in (4, 5, 6, 7))
        accs = [ps[:, 4 + r, :] for r in range(R)]

        s_x = [sem(f"x_loaded{g}") for g in range(2)]
        s_w = sem("weights_loaded")
        s_b = sem("biases_loaded")
        s_ring = [sem(f"ring_loaded{s}") for s in range(SLOTS)]
        s_ring1 = [sem(f"ring_loaded_again{s}") for s in range(SLOTS)]
        s_ident0 = sem("ident_zeroed")
        s_ident = sem("ident_ready")
        s_ones = sem("ones_ready")
        s_wps = sem("weights_transposed")
        s_wsb = sem("weights_ready")
        s_st = sem("layernorm_statistics")
        s_rs0 = sem("h0_scales_ready")
        s_z0 = sem("x_centred")
        s_h0 = sem("h0_ready")
        s_h0hi = sem("h0_hi_ready")
        s_h0lo = sem("h0_lo_ready")
        s_bias = sem("small_constants_ready")
        dve_seq = sem("dve_seq")
        dve_gru = sem("dve_gru")
        dve_norm = sem("dve_norm")
        dve_out = sem("dve_out")
        pool_seq = sem("pool_seq")
        s_t = sem("pair_transposed")
        s_w32 = sem("whole_ready")
        s_tn = sem("pair_turned")
        s_ts = sem("turned_scaled")
        s_hi = sem("adj_hi_ready")
        s_lo = sem("adj_lo_ready")
        s_agg = sem("pair_aggregated")
        s_mxd = sem("row_maxima_taken")
        s_aggT = sem("agg_evacuated")
        s_hst = sem("h_staged")
        s_hTps = sem("h_transposed")
        s_hT = sem("hT_ready")
        s_mps = sem("msg_product")
        s_msg = sem("msg_ready")
        s_rzps = sem("rz_products")
        s_rz = sem("rz_ready")
        s_nps = sem("n_products")
        s_tT = sem("n_argument_ready")
        s_nT = sem("n_ready")
        s_g = sem("gru_ready")
        s_gps = sem("gru_transposed")
        s_x1 = sem("x1_ready")
        s_z1 = sem("z1_ready")
        s_rs = sem("h1_scales_ready")
        s_h1 = sem("h1_ready")
        s_n2 = sem("norms_ready")
        s_h1n = sem("h1_normalised")
        s_qps = sem("q_transposed")
        s_qk = sem("qk_hi_ready")
        s_vh = sem("vals_hi_ready")
        s_qkl = sem("qk_lo_ready")
        s_vl = sem("vals_lo_ready")
        s_m = sem("row_max_ready")
        s_ma = sem("mask_taken")
        s_mk = sem("mask_ready")
        s_s = sem("logits_ready")
        s_p = sem("probs_ready")
        s_pl = sem("probs_lo_ready")
        s_pv = sem("probs_used")
        s_acc = sem("acc_evacuated")
        s_out = sem("out_stored")

        def even(p):
            return p % 4 < 2

        def n_of(p):
            return p // 4 * 2 + p % 2

        ODD = [p for p in range(NPAIR) if not even(p)]
        GATE = 14

        def nth(c, p):
            return NPAIR // 2 * c + n_of(p)

        block = ctx.enter_context(nc.Block())

        @block.sync
        def _(sp):
            def load(c, pc, waits, layer):
                for semaphore, value in waits:
                    sp.wait_ge(semaphore, value)
                slot = pc % SLOTS
                if layer == 0 and pc % 2:
                    for a in range(4):
                        sp.dma_start(ring_q[slot][QD * a:QD * (a + 1), :, :],
                                     adj_q[c, pc, a, :, :, :]).then_inc(s_ring[slot], 16)
                else:
                    sp.dma_start(ring[:, slot, :, :], adj_v[:, c, :, pc * PIECE:(pc + 1) * PIECE])\
                      .then_inc((s_ring1 if layer else s_ring)[slot], 16)

            def free0(c, pc):
                return [(s_mxd, NP * c + pc + 1)]

            def free1(c, pc):
                return [(s_ma, NP * c + pc + 1)]

            def before(c, pc, free):
                return free(c - 1, pc + NP - SLOTS) if pc < SLOTS else free(c, pc - SLOTS)

            for pc in range(NP):
                load(0, pc, before(0, pc, free0) if pc >= SLOTS else [], 0)
            with sp.Fori(1, NC) as c:
                for pc in range(NP):
                    load(c, pc, before(c, pc, free0), 0)
            for pc in range(NP):
                load(0, pc, before(0, pc, free1) if pc >= SLOTS else free0(NC - 1, pc + NP - SLOTS), 1)
            def store(c):
                sp.wait_ge(s_acc, R * (c + 1))
                sp.dma_start(out_v[:, c, :, :], o_st[:, :, :]).then_inc(s_out, 16)

            with sp.Fori(1, NC) as c:
                for pc in range(NP):
                    if pc == 6:
                        store(c - 1)
                    load(c, pc, before(c, pc, free1), 1)
            store(NC - 1)
            sp.wait_ge(s_out, 16 * NC)

        @block.gpsimd
        def _(pool):
            seq = [0]

            def link(ins):
                seq[0] += 1
                ins.then_inc(pool_seq, 1)
                pool.wait_ge(pool_seq, seq[0])

            nc.gpsimd.memset(ident[:, :], 0.0).then_inc(s_ident0, 1)
            pool.wait_ge(s_ident0, 1)
            nc.gpsimd.affine_select(out=ident[:, :], in_=ident[:, :], compare_op=ALU.not_equal, fill=1.0,
                                    base=0, pattern=[[-1, P]], channel_multiplier=1).then_inc(s_ident, 1)
            nc.gpsimd.memset(vals[:, :, 2 * D:2 * D + 1], H_SCALE).then_inc(s_ones, 1)

            def lo(c, p):
                n = nth(c, p)
                b = n_of(p) % NSPLIT
                pool.wait_ge(s_hi, n + 1)
                nc.gpsimd.tensor_tensor(split_lo[:, b, :], turned[:, n_of(p) % NTURN, :, :].rearrange("p j n -> p (j n)"),
                                        split_hi[:, b, :], ALU.subtract).then_inc(s_lo, 1)

            def scale_h0(m):
                pool.wait_ge(s_z0, m + 1)
                pool.wait_ge(s_rs0, min(m, 1) + 1)
                s8 = slice(8 * m, 8 * m + 8)
                nc.gpsimd.tensor_tensor(h0[:, s8, :], h0[:, s8, :], rs[:, s8].unsqueeze(2).broadcast_to([P, 8, D]),
                                        ALU.mult).then_inc(s_h0, 1)

            def stage_h(g):
                pool.wait_ge(s_h0, NGRP)
                nc.gpsimd.tensor_copy(h_st[:, :, :], h0[:, bass.ds(g * R, R), :]).then_inc(s_hst, 1)

            def gate(g, base):
                pool.wait_ge(s_nT, g + 1)
                nc.gpsimd.tensor_tensor(dT[:, :], hT[:, :], nT[:, :], ALU.subtract).then_inc(pool_seq, 1)
                pool.wait_ge(pool_seq, base + 1)
                nc.gpsimd.tensor_tensor(dT[:, :], dT[:, :], zT[:, :], ALU.mult).then_inc(pool_seq, 1)
                pool.wait_ge(pool_seq, base + 2)
                nc.gpsimd.tensor_tensor(dT[:, :], dT[:, :], nT[:, :], ALU.add).then_inc(s_g, 1)

            def h1(g):
                pool.wait_ge(s_rs, g + 1)
                nc.gpsimd.tensor_tensor(h1s[:, :, :], z1[:, :, :], h_scale[:, :].unsqueeze(2).broadcast_to([P, R, D]),
                                        ALU.mult).then_inc(s_h1, 1)

            def vals_lo(g):
                pool.wait_ge(s_vh, g + 1)
                nc.gpsimd.tensor_tensor(vals[:, bass.ds(g * R, R), 0:D], h1s[:, :, :],
                                        vals[:, bass.ds(g * R, R), D:2 * D], ALU.subtract).then_inc(s_vl, 1)

            scale_h0(0)
            for p in ODD:
                lo(0, p)
                if p == 3:
                    for m in range(1, NGRP):
                        scale_h0(m)
            stage_h(0)

            def chunk0(c, older):
                for p in ODD:
                    if p == GATE:
                        gate(c - 1, 2 * (c - 1))
                    lo(c, p)
                    if older and p == 7:
                        h1(c - 2)
                    if older and p == 11:
                        vals_lo(c - 2)
                stage_h(c)

            chunk0(1, False)
            with pool.Fori(2, NC) as c:
                chunk0(c, True)
            h1(NC - 2)
            vals_lo(NC - 2)
            gate(NC - 1, 2 * (NC - 1))
            h1(NC - 1)
            vals_lo(NC - 1)

        @block.scalar
        def _(act):
            for part, (b0, b1) in enumerate(((0, 2), (2, NC))):
                act.dma_start(xs[:, R * b0:R * b1, :].rearrange("p (b j) d -> p b (j d)", j=R),
                              x_v[:, b0:b1, :]).then_inc(s_x[part], 16)
            act.dma_start(w_nat[:, 0, :], W_msg).then_inc(s_w, 16)
            act.dma_start(w_nat[:, 1:4, :], W_ih.rearrange("(g e) d -> e g d", g=3)).then_inc(s_w, 16)
            act.dma_start(w_nat[:, 4:7, :], W_hh.rearrange("(g e) d -> e g d", g=3)).then_inc(s_w, 16)
            act.dma_start(b_m[:, :], b_msg.rearrange("(e a) -> e a", a=1)).then_inc(s_b, 16)
            act.dma_start(b_i[:, :], b_ih.rearrange("(g e) -> e g", g=3),
                          allow_slow_non_contiguous=True).then_inc(s_b, 16)
            act.dma_start(b_h[:, :], b_hh.rearrange("(g e) -> e g", g=3),
                          allow_slow_non_contiguous=True).then_inc(s_b, 16)
            act.dma_start(bt[:, :], beta.partition_broadcast(P)).then_inc(s_b, 16)
            act.wait_ge(s_wps, 1)
            nc.scalar.activation(wT[:, 0:4, :], ps[:, 6, :].rearrange("p (g n) -> p g n", g=4),
                                 ACT.Copy).then_inc(s_wsb, 1)
            nc.scalar.activation(wT[:, 4:7, :], ps[:, 7, 0:3 * P].rearrange("p (g n) -> p g n", g=3),
                                 ACT.Copy).then_inc(s_wsb, 1)

            def h_z(m):
                act.wait_ge(s_st, min(m, 1) + 1)
                for t in range(8 * m, 8 * m + 8):
                    last = nc.scalar.activation(h0[:, t, :], xs[:, t, :], ACT.Relu, bias=neg_mean[:, t:t + 1])
                last.then_inc(s_z0, 1)

            def h_hi(m):
                act.wait_ge(s_h0, m + 1)
                nc.scalar.activation(h0_hi[:, 4 * m:4 * m + 4, :], h0[:, 8 * m + 4:8 * m + 8, :], ACT.Copy,
                                     scale=H_SCALE).then_inc(s_h0hi, 1)

            def evacuate(c, p):
                n = nth(c, p)
                if even(p):
                    b = n_of(p) % NWHOLE
                    act.wait_ge(s_t, n + 1)
                    if p >= 4 or not (isinstance(c, int) and c == 0):
                        act.wait_ge(s_agg, NPAIR * c + p - 3)
                    nc.scalar.activation(whole[:, b, :], tile2[p % 2], ACT.Copy,
                                         scale=A_SCALE * H_SCALE).then_inc(s_w32, 1)
                else:
                    t, b = n_of(p) % NTURN, n_of(p) % NSPLIT
                    pair = turned[:, t, :, :].rearrange("p j n -> p (j n)")
                    act.wait_ge(s_tn, n + 1)
                    nc.scalar.activation(pair, pair, ACT.Copy, scale=A_SCALE).then_inc(s_ts, 1)
                    act.wait_ge(s_ts, n + 1)
                    if p >= 10 or not (isinstance(c, int) and c == 0):
                        act.wait_ge(s_agg, NPAIR * c + p - 7)
                    nc.scalar.activation(split_hi[:, b, :], pair, ACT.Copy).then_inc(s_hi, 1)

            def take_agg(g):
                act.wait_ge(s_agg, NPAIR * (g + 1))
                nc.scalar.activation(aggT[:, :], AGG, ACT.Copy, scale=1.0 / (H_SCALE * A_SCALE)).then_inc(s_aggT, 1)

            def take_qk(g):
                act.wait_ge(s_qps, g + 1)
                nc.scalar.activation(q_hi[:, bass.ds(g * CH, CH)], G6, ACT.Copy, scale=Q_SCALE)
                nc.scalar.activation(k_hi[:, bass.ds(g * CH, CH)], G6, ACT.Copy,
                                     scale=k_scale[:, :]).then_inc(s_qk, 1)

            def gru(g, p):
                if p == 4:
                    act.wait_ge(s_hTps, g + 1)
                    nc.scalar.activation(hT[:, :], G5, ACT.Copy).then_inc(s_hT, 1)
                    act.wait_ge(s_mps, g + 1)
                    nc.scalar.activation(msgT[:, :], G7, ACT.Relu, bias=b_m[:, :]).then_inc(s_msg, 1)
                if p == 8:
                    act.wait_ge(s_rzps, g + 1)
                    nc.scalar.activation(rT[:, :], G7, ACT.Sigmoid, bias=b_rz[:, 0:1])
                    nc.scalar.activation(zT[:, :], G5, ACT.Sigmoid, bias=b_rz[:, 1:2]).then_inc(s_rz, 1)
                if p == 11:
                    act.wait_ge(s_tT, g + 1)
                    nc.scalar.activation(nT[:, :], tT[:, :], ACT.Tanh, bias=b_i[:, 2:3]).then_inc(s_nT, 1)

            def late(g, p):
                if p == 2:
                    act.wait_ge(s_z1, g + 1)
                    for r in range(R):
                        last = nc.scalar.activation(sq[:, r, :], z1[:, r, :], ACT.Square, accum_out=n2[:, r:r + 1])
                    last.then_inc(s_n2, 1)
                if p == 7:
                    take_qk(g)
                if p == 9:
                    act.wait_ge(s_h1, g + 1)
                    nc.scalar.activation(vals[:, bass.ds(g * R, R), D:2 * D], h1s[:, :, :], ACT.Copy).then_inc(s_vh, 1)

            h_z(0)
            for p in range(NPAIR):
                evacuate(0, p)
                if p == 1:
                    h_hi(0)
                if p == 2:
                    for m in range(1, NGRP):
                        h_z(m)
                if p in (4, 6, 8):
                    h_hi(p // 2 - 1)
            evacuate(1, 0)
            evacuate(1, 1)
            act.wait_ge(s_bias, 1)
            take_agg(0)

            def chunk0(c, older, final):
                for p in range(2, NPAIR):
                    evacuate(c, p)
                    gru(c - 1, p)
                    if older:
                        late(c - 2, p)
                if not final:
                    evacuate(c + 1, 0)
                    evacuate(c + 1, 1)
                take_agg(c)

            chunk0(1, False, False)
            with act.Fori(2, NC - 1) as c:
                chunk0(c, True, False)
            chunk0(NC - 1, True, True)
            for p in range(2, NPAIR):
                gru(NC - 1, p)
                late(NC - 2, p)
            for p in range(2, NPAIR):
                late(NC - 1, p)

            def probs(c, n):
                U = NK * c + n
                act.wait_ge(s_s, U + 1)
                if not (isinstance(c, int) and U < NB):
                    act.wait_ge(s_pv, U - NB + 1)
                nc.scalar.activation(p_hi[:, n % NB, :], ps[:, n % NB, :], ACT.Exp,
                                     bias=p_bias[:, :], scale=1.0 / L_SCALE)
                nc.scalar.activation(ps[:, n % NB, :], ps[:, n % NB, :], ACT.Exp,
                                     bias=p_bias[:, :], scale=1.0 / L_SCALE).then_inc(s_p, 1)

            for n in range(NK):
                probs(0, n)
            with act.Fori(1, NC) as c:
                for n in range(NK):
                    probs(c, n)

        @block.vector
        def _(dve):
            seq = [0]

            def link(ins):
                seq[0] += 1
                ins.then_inc(dve_seq, 1)
                dve.wait_ge(dve_seq, seq[0])

            def rsqrt(y, a, t, h, chain):
                chain(nc.vector.tensor_scalar(y.bitcast(i32), a.bitcast(i32), -0.5, float(0x5F3759DF), ALU.mult, ALU.add))
                chain(nc.vector.tensor_scalar(h, a, -0.5, None, ALU.mult))
                for _ in range(3):
                    chain(nc.vector.tensor_tensor(t, y, y, ALU.mult))
                    chain(nc.vector.tensor_tensor(t, t, h, ALU.mult))
                    chain(nc.vector.scalar_tensor_tensor(out=y, in0=t, scalar=1.5, in1=y, op0=ALU.add, op1=ALU.mult))

            def statistics(t0, t1):
                dve.wait_ge(s_x[1] if t0 else s_x[0], 16)
                for t in range(t0, t1):
                    last = nc.vector.bn_stats(stats[:, t, :], xs[:, t, :])
                link(last)
                for t in range(t0, t1):
                    last = nc.vector.bn_aggr(mv[:, t, :], stats[:, t, :])
                link(last)
                s8 = slice(t0, t1)
                nc.vector.tensor_scalar(neg_mean[:, s8], mv[:, s8, 0], -1.0, None, ALU.mult).then_inc(s_st, 1)
                link(nc.vector.tensor_scalar(va[:, s8], mv[:, s8, 1], LN_EPS, None, ALU.add))
                rsqrt(rs[:, s8], va[:, s8], nt1[:, s8], nt2[:, s8], link)
                nc.vector.tensor_scalar(rs[:, s8], rs[:, s8], 1.0, None, ALU.mult).then_inc(s_rs0, 1)

            def h_lo(m):
                dve.wait_ge(s_h0hi, m + 1)
                nc.vector.scalar_tensor_tensor(out=h0_lo[:, 4 * m:4 * m + 4, :], in0=h0[:, 8 * m + 4:8 * m + 8, :],
                                               scalar=H_SCALE, in1=h0_hi[:, 4 * m:4 * m + 4, :],
                                               op0=ALU.mult, op1=ALU.subtract).then_inc(s_h0lo, 1)

            def turn(c, p):
                n, pc, j0 = nth(c, p), p // 2, 2 * (p % 2)
                if p % 2 == 0:
                    dve.wait_ge(s_ring[pc % SLOTS], 64 * (2 * c + 1 + pc // SLOTS))
                if p >= 6 or not (isinstance(c, int) and c == 0):
                    dve.wait_ge(s_lo, n - NTURN + 1)
                nc.vector.transpose(turned[:, n_of(p) % NTURN, :, :],
                                    ring_q[pc % SLOTS].rearrange("p g (c j) -> p j g c", c=QD)
                                    [:, j0:j0 + 2, :, :]).then_inc(s_tn, 1)

            def row_max(c, pc):
                if pc % 2 == 0:
                    dve.wait_ge(s_t, nth(c, 2 * pc + 1) + 1)
                    nc.vector.tensor_reduce(mx[:, pc // 2, bass.ds(c, 1), :].rearrange("p a r -> p (a r)"),
                                            ring[:, pc % SLOTS, :, :], AX.X, ALU.max).then_inc(s_mxd, 1)
                else:
                    nc.vector.tensor_reduce(mxq[:, pc // 2, bass.ds(c * G, G)], ring_q[pc % SLOTS], AX.X,
                                            ALU.max).then_inc(s_mxd, 1)

            LINKS, NORM_LINKS = 3, 12

            def gru(g, stage):
                done = [1 if stage == "x1" else 0]

                def link_g(ins):
                    done[0] += 1
                    ins.then_inc(dve_gru, 1)
                    dve.wait_ge(dve_gru, LINKS * g + done[0])

                def link_n(ins):
                    done[0] += 1
                    ins.then_inc(dve_norm, 1)
                    dve.wait_ge(dve_norm, NORM_LINKS * g + done[0])

                if stage == "t":
                    dve.wait_ge(s_nps, g + 1)
                    link_g(nc.vector.scalar_tensor_tensor(out=tT[:, :], in0=G6, scalar=b_h[:, 2:3], in1=rT[:, :],
                                                          op0=ALU.add, op1=ALU.mult))
                    nc.vector.tensor_tensor(tT[:, :], G7, tT[:, :], ALU.add).then_inc(s_tT, 1)
                if stage == "x1":
                    x1 = xs[:, bass.ds(g * R, R), :]
                    dve.wait_ge(s_gps, g + 1)
                    nc.vector.tensor_tensor(x1_st[:, :, :], G5.rearrange("p (r d) -> p r d", r=R), x1,
                                            ALU.add).then_inc(s_x1, 1)
                    dve.wait_ge(s_x1, g + 1)
                    nc.vector.tensor_scalar(xs[:, bass.ds(g * R, 2), :], x1_st[:, 0:2, :], 1.0, None, ALU.mult)
                    for r in range(R):
                        last = nc.vector.bn_stats(stats[:, r, :], x1_st[:, r, :])
                    link_g(last)
                    nc.vector.tensor_scalar(xs[:, bass.ds(g * R + 2, 2), :], x1_st[:, 2:4, :], 1.0, None, ALU.mult)
                    for r in range(R):
                        last = nc.vector.bn_aggr(mv[:, r, :], stats[:, r, :])
                    link_g(last)
                    for r in range(R):
                        last = nc.vector.tensor_scalar(z1[:, r, :], x1_st[:, r, :], mv[:, r, 0:1], 0.0,
                                                       ALU.subtract, ALU.max)
                    last.then_inc(s_z1, 1)
                    nc.vector.tensor_scalar(va2[:, 0:R], mv[:, 0:R, 1], LN_EPS, None, ALU.add)
                if stage == "norm":
                    dve.wait_ge(s_n2, g + 1)
                    link_n(nc.vector.tensor_scalar(va2[:, R:2 * R], n2[:, :], 1e-30, None, ALU.max))
                    rsqrt(rs2[:, :], va2[:, :], c1[:, :], c2[:, :], link_n)
                    nc.vector.tensor_scalar(h_scale[:, :], rs2[:, 0:R], H_SCALE, None, ALU.mult).then_inc(s_rs, 1)
                    for r in range(R):
                        last = nc.vector.tensor_scalar(h1n[:, r, :], z1[:, r, :], rs2[:, R + r:R + r + 1], None,
                                                       ALU.mult)
                    last.then_inc(s_h1n, 1)
                if stage == "qk":
                    dve.wait_ge(s_qk, g + 1)
                    cols = bass.ds(g * CH, CH)
                    nc.vector.scalar_tensor_tensor(out=q_lo[:, cols], in0=G6, scalar=Q_SCALE, in1=q_hi[:, cols],
                                                   op0=ALU.mult, op1=ALU.subtract)
                    nc.vector.scalar_tensor_tensor(out=k_lo[:, cols], in0=G6, scalar=k_scale[:, :], in1=k_hi[:, cols],
                                                   op0=ALU.mult, op1=ALU.subtract).then_inc(s_qkl, 1)

            statistics(0, 8)
            turn(0, 2)
            turn(0, 3)
            statistics(8, NT)
            h_lo(0)
            row_max(0, 0)
            row_max(0, 1)
            for m in range(1, NGRP):
                turn(0, 4 * m + 2)
                row_max(0, 2 * m)
                h_lo(m)
                turn(0, 4 * m + 3)
                row_max(0, 2 * m + 1)
            turn(1, 2)
            dve.wait_ge(s_b, 64)
            nc.vector.tensor_tensor(b_rz[:, :], b_i[:, 0:2], b_h[:, 0:2], ALU.add)
            nc.vector.tensor_scalar(k_scale[:, :], bt[:, :], Q_SCALE, None, ALU.mult)
            link(nc.vector.tensor_scalar(bt_neg[:, :], bt[:, :], -1.0, None, ALU.mult))
            link(nc.vector.tensor_tensor(p_bias[:, :], bt[:, :], bt_neg[:, :], ALU.max))
            nc.vector.tensor_scalar(p_bias[:, :], p_bias[:, :], -1.0, P_LOG_SCALE, ALU.mult, ALU.add).then_inc(s_bias, 1)

            def chunk0(c, older, final):
                row_max(c, 0)
                turn(c, 3)
                row_max(c, 1)
                turn(c, 6)
                if older:
                    gru(c - 2, "norm")
                row_max(c, 2)
                turn(c, 7)
                row_max(c, 3)
                turn(c, 10)
                row_max(c, 4)
                if older:
                    gru(c - 2, "qk")
                turn(c, 11)
                row_max(c, 5)
                gru(c - 1, "t")
                turn(c, 14)
                row_max(c, 6)
                turn(c, 15)
                row_max(c, 7)
                if not final:
                    turn(c + 1, 2)
                gru(c - 1, "x1")

            chunk0(1, False, False)
            with dve.Fori(2, NC - 1) as c:
                chunk0(c, True, False)
            chunk0(NC - 1, True, True)

            dve.wait_ge(s_mxd, NP * NC)
            link(nc.vector.tensor_reduce(mxo[:, :], mxq[:, :, :].rearrange("p h t -> p t h"), AX.X, ALU.max))
            mo = mxo[:, :].rearrange("p (c r q) -> p c r q", c=NC, r=R)
            for a in range(4):
                for q in range(4):
                    last = nc.vector.tensor_scalar(mx[QD * q:QD * (q + 1), 4 + a, :, :],
                                                   mo[QD * a:QD * (a + 1), :, :, q], 1.0, None, ALU.mult)
            link(last)
            link(nc.vector.tensor_reduce(m_row[:, :], mx[:, :, :, :].rearrange("p h c r -> p (c r) h"), AX.X, ALU.max))
            link(nc.vector.tensor_scalar(m_row[:, :], m_row[:, :], -1.0, NEG * L_SCALE, ALU.add, ALU.mult))
            for g, stage in ((NC - 2, "norm"), (NC - 2, "qk"), (NC - 1, "t"), (NC - 1, "x1"), (NC - 1, "norm"),
                             (NC - 1, "qk")):
                gru(g, stage)

            def mask(c, pc, part):
                buf = pc % 2
                if part == 0:
                    dve.wait_ge(s_ring1[pc % SLOTS], 16 * (2 * c + 1 + pc // SLOTS))
                    nc.vector.tensor_scalar(masks[:, buf, :, :], ring[:, pc % SLOTS, :, :], -1.0, NEG * L_SCALE,
                                            ALU.add, ALU.mult).then_inc(s_ma, 1)
                    dve.wait_ge(s_ma, NP * c + pc + 1)
                else:
                    for r in (2 * part - 2, 2 * part - 1):
                        last = nc.vector.tensor_scalar(masks[:, buf, r, :], masks[:, buf, r, :],
                                                       m_row[:, bass.ds(c * R + r, 1)], None, ALU.subtract)
                    if part == 2:
                        last.then_inc(s_mk, 1)

            def probs_lo(c, n):
                dve.wait_ge(s_p, NK * c + n + 1)
                nc.vector.tensor_tensor(p_lo[:, n % NB, :], ps[:, n % NB, :], p_hi[:, n % NB, :],
                                        ALU.subtract).then_inc(s_pl, 1)

            def output(c, first):
                dve.wait_ge(s_pv, NK * (c + 1))
                for r in range(R):
                    nc.vector.reciprocal(o_den[:, r:r + 1], accs[r][:, 2 * D:2 * D + 1]).then_inc(dve_out, 1)
                    dve.wait_ge(dve_out, 2 * R * c + 2 * r + 1)
                    nc.vector.scalar_tensor_tensor(out=o_t[:, r, :], in0=accs[r][:, 0:D], scalar=o_den[:, r:r + 1],
                                                   in1=xs[:, bass.ds(c * R + r, 1), :].rearrange("p a d -> p (a d)"),
                                                   op0=ALU.mult, op1=ALU.add).then_inc(dve_out, 1)
                    dve.wait_ge(dve_out, 2 * R * c + 2 * r + 2)
                    if r == 0 and not first:
                        dve.wait_ge(s_out, 16 * c)
                    nc.vector.scalar_tensor_tensor(out=o_st[:, r, :], in0=accs[r][:, D:2 * D], scalar=o_den[:, r:r + 1],
                                                   in1=o_t[:, r, :], op0=ALU.mult, op1=ALU.add).then_inc(s_acc, 1)

            def chunk(c, first, final):
                for n in range(1, NK + 1):
                    if n < NK:
                        probs_lo(c, n)
                    elif not final:
                        probs_lo(c + 1, 0)
                    m, q = (n - 1) // KB, (n - 1) % KB
                    if q == 0:
                        dve.wait_ge(s_s, NK * c + KB * (m + 1))
                    if q < 3:
                        if m + 2 < NP:
                            mask(c, m + 2, q)
                        elif not final:
                            mask(c + 1, m + 2 - NP, q)
                output(c, first)

            for pc in range(2):
                for part in range(3):
                    mask(0, pc, part)
            probs_lo(0, 0)
            chunk(0, True, False)
            with dve.Fori(1, NC - 1) as c:
                chunk(c, False, False)
            chunk(NC - 1, False, True)

        @block.tensor
        def _(pe):
            def block_T(dst, src, first=True):
                return nc.tensor.matmul(dst, lhsT=src, rhs=ident[:, :], start=first, stop=True,
                                        is_transpose=True, skip_group_check=True)

            pe.wait_ge(s_w, 48)
            pe.wait_ge(s_ident, 1)
            for i in range(7):
                last = block_T(ps[:, 6 + i // 4, (i % 4) * P:(i % 4 + 1) * P], w_nat[:, i, :])
            last.then_inc(s_wps, 1)

            def transposes(c, p):
                n, pc = nth(c, p), p // 2
                if p % 2 == 0:
                    pe.wait_ge(s_ring[pc % SLOTS], 16 * (2 * c + 1 + pc // SLOTS))
                if p >= 4 or not (isinstance(c, int) and c == 0):
                    pe.wait_ge(s_w32, n - 1)
                for b in range(2):
                    for r in range(R):
                        last = block_T(tile2[p % 2][:, b * CH + r * P:b * CH + (r + 1) * P],
                                       tile_cols(ring[:, pc % SLOTS, r, :], 2 * (p % 2) + b))
                last.then_inc(s_t, 1)

            def aggregate(c, p):
                n, first_chunk = nth(c, p), isinstance(c, int) and c == 0
                if first_chunk and p % 2 == 0:
                    pe.wait_ge(s_h0 if even(p) else s_h0lo, p // 4 + 1)
                pe.wait_ge(s_w32 if even(p) else s_lo, n + 1)
                if p == 0 and not first_chunk:
                    pe.wait_ge(s_aggT, c)
                for b in range(2):
                    k, cols = 2 * p + b, slice(b * CH, (b + 1) * CH)
                    first, final = k == 0, k == NK - 1
                    if even(p):
                        last = nc.tensor.matmul(AGG, lhsT=h0[:, k, :], rhs=whole[:, n_of(p) % NWHOLE, cols],
                                                start=first, stop=final)
                    else:
                        ah, al = split_hi[:, n_of(p) % NSPLIT, cols], split_lo[:, n_of(p) % NSPLIT, cols]
                        ko = KB * (p // 4) + k % KB
                        nc.tensor.matmul(AGG, lhsT=h0_hi[:, ko, :], rhs=ah, start=first, stop=False)
                        nc.tensor.matmul(AGG, lhsT=h0_hi[:, ko, :], rhs=al, start=False, stop=False)
                        last = nc.tensor.matmul(AGG, lhsT=h0_lo[:, ko, :], rhs=ah, start=False, stop=final)
                last.then_inc(s_agg, 1)

            def gru(g, p, older=True):
                if p == 1:
                    pe.wait_ge(s_hst, g + 1)
                    if older:
                        pe.wait_ge(s_x1, g)
                    for r in range(R):
                        last = block_T(tile_cols(G5, r), h_st[:, r, :])
                    last.then_inc(s_hTps, 1)
                if p == 2:
                    pe.wait_ge(s_aggT, g + 1)
                    nc.tensor.matmul(G7, lhsT=wT[:, 0, :], rhs=aggT[:, :], start=True, stop=True).then_inc(s_mps, 1)
                if p == 5:
                    pe.wait_ge(s_msg, g + 1)
                    for gate, dst in ((0, G7), (1, G5)):
                        nc.tensor.matmul(dst, lhsT=wT[:, 1 + gate, :], rhs=msgT[:, :], start=True, stop=False)
                        last = nc.tensor.matmul(dst, lhsT=wT[:, 4 + gate, :], rhs=hT[:, :], start=False, stop=True)
                    last.then_inc(s_rzps, 1)
                if p == 8:
                    pe.wait_ge(s_rz, g + 1)
                    if older:
                        pe.wait_ge(s_qkl, g)
                    nc.tensor.matmul(G6, lhsT=wT[:, 6, :], rhs=hT[:, :], start=True, stop=True)
                    nc.tensor.matmul(G7, lhsT=wT[:, 3, :], rhs=msgT[:, :], start=True, stop=True).then_inc(s_nps, 1)
                if p == 12:
                    pe.wait_ge(s_g, g + 1)
                    for r in range(R):
                        last = block_T(G5[:, r * P:(r + 1) * P], tile_cols(dT[:, :], r))
                    last.then_inc(s_gps, 1)

            def late(g, p):
                if p == 4:
                    pe.wait_ge(s_h1n, g + 1)
                    for r in range(R):
                        last = block_T(tile_cols(G6, r), h1n[:, r, :])
                    last.then_inc(s_qps, 1)

            def chunk0(c, age, final):
                for p in range(NPAIR):
                    if even((p + 3) % NPAIR) and not (final and p + 3 >= NPAIR):
                        transposes(c if p + 3 < NPAIR else c + 1, (p + 3) % NPAIR)
                    aggregate(c, p)
                    if age >= 1:
                        gru(c - 1, p, older=age >= 2)
                    if age >= 2:
                        late(c - 2, p)

            pe.wait_ge(s_wsb, 2)
            transposes(0, 0)
            transposes(0, 1)
            chunk0(0, 0, False)
            chunk0(1, 1, False)
            with pe.Fori(2, NC - 1) as c:
                chunk0(c, 2, False)
            chunk0(NC - 1, 2, True)
            for p in range(NPAIR):
                gru(NC - 1, p)
                late(NC - 2, p)
            late(NC - 1, 4)

            def logits(c, n):
                pc, j = n // KB, n % KB
                U = NK * c + n
                if j == 0:
                    pe.wait_ge(s_mk, NP * c + pc + 1)
                if not (isinstance(c, int) and U < NB):
                    pe.wait_ge(s_pl, U - NB + 1)
                bank = ps[:, n % NB, :]
                for r in range(R):
                    block_T(bank[:, r * P:(r + 1) * P], tile_cols(masks[:, pc % 2, r, :], j), first=(r == 0))
                qc = bass.ds(c * CH, CH)
                for kk, qq in ((k_hi, q_hi), (k_hi, q_lo), (k_lo, q_hi)):
                    last = nc.tensor.matmul(bank, lhsT=tile_cols(kk[:, pc * PIECE:(pc + 1) * PIECE], j), rhs=qq[:, qc], start=False, stop=(kk is k_lo),
                                            skip_group_check=True)
                last.then_inc(s_s, 1)

            def weigh(c, n):
                pe.wait_ge(s_pl, NK * c + n + 1)
                for r in range(R):
                    if n == 0:
                        pe.wait_ge(s_acc, R * (c - 1) + r + 1) if not (isinstance(c, int) and c == 0) else None
                    hi = (tile_cols(p_hi[:, n % NB, :], r), 0)
                    lo = (tile_cols(p_lo[:, n % NB, :], r), D)
                    for i, (weights, col) in enumerate((hi, lo) if n == 0 else (lo, hi)):
                        last = nc.tensor.matmul(accs[r][:, col:W], lhsT=weights, rhs=vals[:, n, col:W],
                                                start=(n == 0 and i == 0), stop=(n == NK - 1 and i == 1),
                                                skip_group_check=True)
                last.then_inc(s_pv, 1)

            def chunk1(c, final):
                for n in range(NK):
                    if n + AHEAD < NK:
                        logits(c, n + AHEAD)
                    elif not final:
                        logits(c + 1, n + AHEAD - NK)
                    weigh(c, n)

            pe.wait_ge(s_qkl, NC)
            pe.wait_ge(s_vl, NC)
            pe.wait_ge(s_ones, 1)
            for n in range(AHEAD):
                logits(0, n)
            chunk1(0, False)
            with pe.Fori(1, NC - 1) as c:
                chunk1(c, False)
            chunk1(NC - 1, True)


_INS = ["x", "adj", "L0_gnn_W_msg", "L0_gnn_b_msg", "L0_gnn_W_ih", "L0_gnn_W_hh", "L0_gnn_b_ih", "L0_gnn_b_hh",
        "L1_gnn_beta"]
_OUTS = [((4096, 128), "float32")]


def kernel(**inputs):
    import numpy as _np
    import concourse.bacc as _bacc
    from concourse import mybir as _mybir
    from concourse.bass_utils import run_bass_kernel_spmd as _run

    nc = _bacc.Bacc("TRN2", target_bir_lowering=False, num_devices=1)
    arrays, args = {}, []
    for name in _INS:
        a = _np.ascontiguousarray(inputs[name])
        arrays[f"in_{name}_dram"] = a
        args.append(nc.dram_tensor(f"in_{name}_dram", a.shape, _mybir.dt.from_np(a.dtype), kind="ExternalInput").ap())
    for i, (shape, dtype) in enumerate(_OUTS):
        dt = _mybir.dt.from_np(_np.dtype(dtype))
        args.append(nc.dram_tensor(f"out_{i}_dram", shape, dt, kind="ExternalOutput").ap())
    gnn_gru_then_masked_attention(nc, *args)
    r = _run(nc, [arrays], core_ids=[0])
    return r.results[0]["out_0_dram"]
```

```python
import concourse.bass as bass
from concourse import mybir
from contextlib import ExitStack


def gnn_gru_then_masked_attention(
    nc: bass.Bass,
    x: bass.AP,
    adj: bass.AP,
    W_msg: bass.AP,
    b_msg: bass.AP,
    W_ih: bass.AP,
    W_hh: bass.AP,
    b_ih: bass.AP,
    b_hh: bass.AP,
    beta: bass.AP,
    out: bass.AP,
):
    f32, f16, i32 = mybir.dt.float32, mybir.dt.float16, mybir.dt.int32
    ALU = mybir.AluOpType
    ACT = mybir.ActivationFunctionType
    AX = mybir.AxisListType

    N, D = x.shape
    P = 128
    QD = 32
    G = 16
    NT = N // P
    R = 4
    CH = R * P
    NC = N // CH
    PIECE = 512
    NP = N // PIECE
    KB = PIECE // P
    NK = N // P
    SLOTS = 4
    NPAIR = NK // 2
    NGRP = 4
    NWHOLE, NTURN, NSPLIT = 2, 2, 4
    AHEAD = 3
    NB = 4
    W = 2 * D + 1

    LN_EPS = 1e-5
    EPS = 1e-7
    NORM_INV_MAX = 0.7071
    NEG = 1e9
    H_SCALE = 2.0 ** 8
    A_SCALE = 2.0 ** 10
    Q_SCALE = 2.0 ** 8
    L_SCALE = Q_SCALE * Q_SCALE
    P_LOG_SCALE = 6.931471805599453

    adj_v = adj.rearrange("(c r p) k -> p c r k", p=P, r=R)
    adj_q = adj.rearrange("(c g r) (b a m) -> c b a r g m", r=QD, g=G, a=4, m=P)
    x_v = x.rearrange("(b p j) d -> p b (j d)", p=P, j=R)
    out_v = out.rearrange("(b p j) d -> p b j d", p=P, j=R)

    def tile_cols(ap, j):
        return ap.rearrange("p (i j) -> p j i", j=R)[:, j, :]

    ctx = ExitStack()
    with ctx:
        def sb(name, shape, dt):
            return ctx.enter_context(nc.sbuf_tensor(name, shape, dt))

        def sem(name):
            return ctx.enter_context(nc.semaphore(name))

        ring = sb("adj_ring", [P, SLOTS, R, PIECE], f32)
        xs = sb("xs", [P, NT, D], f32)
        h0 = sb("h0", [P, NT, D], f32)
        h0_hi = sb("h0_hi", [P, NT // 2, D], f16)
        h0_lo = sb("h0_lo", [P, NT // 2, D], f16)
        whole = sb("whole", [P, NWHOLE, 2 * CH], f32)
        turned = sb("turned", [P, NTURN, 2, CH], f32)
        split_hi = sb("split_hi", [P, NSPLIT, 2 * CH], f16)
        split_lo = sb("split_lo", [P, NSPLIT, 2 * CH], f16)
        q_hi = sb("q_hi", [P, N], f16)
        q_lo = sb("q_lo", [P, N], f16)
        k_hi = sb("k_hi", [P, N], f16)
        k_lo = sb("k_lo", [P, N], f16)
        vals = sb("vals", [P, NT, W + 1], f16)
        w_nat = sb("w_nat", [P, 7, D], f32)
        wT = sb("wT", [P, 7, D], f32)
        ident = sb("ident", [P, P], f32)
        b_m = sb("b_m", [P, 1], f32)
        b_i = sb("b_i", [P, 3], f32)
        b_h = sb("b_h", [P, 3], f32)
        b_rz = sb("b_rz", [P, 2], f32)
        bt = sb("bt", [P, 1], f32)
        bt_neg = sb("bt_neg", [P, 1], f32)
        k_scale = sb("k_scale", [P, 1], f32)
        p_bias = sb("p_bias", [P, 1], f32)
        stats = sb("stats", [P, NT, 6], f32)
        mv = sb("mv", [P, NT, 2], f32)
        va = sb("va", [P, NT], f32)
        rs = sb("rs", [P, NT], f32)
        nt1 = sb("nt1", [P, NT], f32)
        nt2 = sb("nt2", [P, NT], f32)
        mx = sb("mx", [P, NP, NC, R], f32)
        mxq = sb("mxq", [P, NP // 2, NC * G], f32)
        m_row = sb("m_row", [P, NT], f32)
        h_st = sb("h_st", [P, R, D], f32)
        hT = sb("hT", [P, CH], f32)
        aggT = sb("aggT", [P, CH], f32)
        msgT = sb("msgT", [P, CH], f32)
        rT = sb("rT", [P, CH], f32)
        zT = sb("zT", [P, CH], f32)
        tT = sb("tT", [P, CH], f32)
        nT = sb("nT", [P, CH], f32)
        dT = sb("dT", [P, CH], f32)
        x1_st = sb("x1_st", [P, R, D], f32)
        z1 = sb("z1", [P, R, D], f32)
        h1s = sb("h1s", [P, R, D], f32)
        h1n = sb("h1n", [P, R, D], f32)
        neg_mean = sb("neg_mean", [P, NT], f32)
        h_scale = sb("h_scale", [P, R], f32)
        mxo = sb("mxo", [P, NC * G], f32)
        sq = sb("sq", [P, R, D], f32)
        n2 = sb("n2", [P, R], f32)
        va2 = sb("va2", [P, 2 * R], f32)
        rs2 = sb("rs2", [P, 2 * R], f32)
        c1 = sb("c1", [P, 2 * R], f32)
        c2 = sb("c2", [P, 2 * R], f32)
        p_hi = sb("p_hi", [P, NB, CH], f16)
        p_lo = sb("p_lo", [P, NB, CH], f16)
        m_quad = sb("m_quad", [P, NC, G], f32)
        m_now = sb("m_now", [P, G], f32)
        minus_one = sb("minus_one", [P, 1], f32)
        norm_inv = sb("norm_inv", [P, NT], f32)
        norm_t = sb("norm_t", [P, R], f32)
        worst = sb("worst", [P, QD], f32)
        worst_t = sb("worst_t", [P, QD], f32)
        flag = sb("flag", [P, 1], i32)
        idle_v = sb("idle_v", [P, 1], f32)
        idle = sb("idle", [P, NP + 1], f32)
        sums = sb("sums", [P, R, W], f32)
        o_den = sb("o_den", [P, R], f32)
        o_t, o_st = x1_st, h_st
        masks = h0[:, :, :].rearrange("p (s r q) d -> p s r (q d)", s=2, r=R)

        ring_q = [ring[:, s, :, :].rearrange("p r n -> p (r n)").rearrange("p (g m) -> p g m", g=G)
                  for s in range(SLOTS)]
        turned_mask = turned[:, :, :, :].rearrange("p a b n -> p (a b) n")
        ps = ctx.enter_context(nc.psum_tensor("ps", [P, 8, 512], f32))
        tile2 = [ps[:, 2 * b:2 * b + 2, :].rearrange("p a n -> p (a n)") for b in range(2)]
        AGG, G5, G6, G7 = (ps[:, b, :] for b in (4, 5, 6, 7))
        accs = [ps[:, 4 + r, :] for r in range(R)]

        s_x = [sem(f"x_loaded{g}") for g in range(3)]
        s_w = sem("weights_loaded")
        s_b = sem("biases_loaded")
        s_ring = [sem(f"ring_loaded{s}") for s in range(SLOTS)]
        s_ring1 = [sem(f"ring_loaded_again{s}") for s in range(SLOTS)]
        s_ident0 = sem("ident_zeroed")
        s_ident = sem("ident_ready")
        s_ones = sem("ones_ready")
        s_wps = sem("weights_transposed")
        s_wsb = sem("weights_ready")
        s_st = sem("layernorm_statistics")
        s_rs0 = sem("h0_scales_ready")
        s_z0 = sem("x_centred")
        s_h0 = sem("h0_ready")
        s_h0hi = sem("h0_hi_ready")
        s_h0lo = sem("h0_lo_ready")
        s_bias = sem("small_constants_ready")
        dve_seq = sem("dve_seq")
        dve_gru = sem("dve_gru")
        dve_norm = sem("dve_norm")
        pool_seq = sem("pool_seq")
        pool_out = sem("pool_out")
        pool_mask = sem("pool_mask")
        s_t = sem("pair_transposed")
        s_w32 = sem("whole_ready")
        s_tn = sem("pair_turned")
        s_ts = sem("turned_scaled")
        s_hi = sem("adj_hi_ready")
        s_lo = sem("adj_lo_ready")
        s_agg = sem("pair_aggregated")
        s_mxd = sem("row_maxima_taken")
        s_aggT = sem("agg_evacuated")
        s_hst = sem("h_staged")
        s_hTps = sem("h_transposed")
        s_hT = sem("hT_ready")
        s_mps = sem("msg_product")
        s_msg = sem("msg_ready")
        s_rzps = sem("rz_products")
        s_rz = sem("rz_ready")
        s_nps = sem("n_products")
        s_tT = sem("n_argument_ready")
        s_nT = sem("n_ready")
        s_g = sem("gru_ready")
        s_gps = sem("gru_transposed")
        s_x1 = sem("x1_ready")
        s_z1 = sem("z1_ready")
        s_rs = sem("h1_scales_ready")
        s_h1 = sem("h1_ready")
        s_n2 = sem("norms_ready")
        s_h1n = sem("h1_normalised")
        s_qps = sem("q_transposed")
        s_qk = sem("qk_hi_ready")
        s_vh = sem("vals_hi_ready")
        s_qkl = sem("qk_lo_ready")
        s_vl = sem("vals_lo_ready")
        s_m = sem("row_max_ready")
        s_ma = sem("mask_taken")
        s_mk = sem("mask_ready")
        s_mq = sem("odd_mask_ready")
        s_tm = sem("mask_tile_turned")
        s_am = sem("mask_added")
        s_s = sem("logits_ready")
        s_p = sem("probs_ready")
        s_pl = sem("probs_lo_ready")
        s_pv = sem("probs_used")
        s_accd = sem("acc_evacuated_by_dve")
        s_acca = sem("acc_evacuated_by_act")
        s_den = sem("denominators_inverted")
        s_o = sem("output_staged")
        s_out = sem("out_stored")
        s_flag = sem("eps_flag_ready")
        pool_norm = sem("pool_norm")
        dve_gen = sem("gen_dve")
        s_gring = sem("gen_ring_loaded")
        s_gma = sem("gen_mask_taken")
        s_gmk = sem("gen_mask_ready")
        s_gdiag = sem("gen_diagonals_ready")
        s_gbc = sem("gen_norms_broadcast")
        s_gs = sem("gen_products_ready")
        s_gl = sem("gen_logits_ready")
        s_gp = sem("gen_probs_ready")
        s_gpl = sem("gen_probs_lo_ready")
        s_gpv = sem("gen_probs_used")
        s_gacc = sem("gen_acc_evacuated")
        s_go = sem("gen_output_staged")

        def even(p):
            return p % 4 < 2

        def n_of(p):
            return p // 4 * 2 + p % 2

        ODD = [p for p in range(NPAIR) if not even(p)]
        GATE = 14
        GATE_T = 13

        def nth(c, p):
            return NPAIR // 2 * c + n_of(p)

        LESS_AT = (6, 0, 2, 3)
        SCALE_AT = (6, 0, 2, 4)

        def tile_of(n):
            return n // 8 * 2 + n % 2, n % 8 // 2, n % 2 == 1

        block = ctx.enter_context(nc.Block())

        @block.sync
        def _(sp):
            def load(c, pc, waits, layer):
                for semaphore, value in waits:
                    sp.wait_ge(semaphore, value)
                slot = pc % SLOTS
                if pc % 2:
                    for a in range(4):
                        sp.dma_start(ring_q[slot][QD * a:QD * (a + 1), :, :],
                                     adj_q[c, pc, a, :, :, :]).then_inc((s_ring1 if layer else s_ring)[slot], 16)
                else:
                    sp.dma_start(ring[:, slot, :, :], adj_v[:, c, :, pc * PIECE:(pc + 1) * PIECE])\
                      .then_inc((s_ring1 if layer else s_ring)[slot], 16)

            def free0(c, pc):
                return [(s_mxd, NP * c + pc + 1)]

            def free1(c, pc):
                return [(s_tm if pc % 2 else s_ma, NK // 2 * c + KB * (pc // 2 + 1))]

            def before(c, pc, free):
                return free(c - 1, pc + NP - SLOTS) if pc < SLOTS else free(c, pc - SLOTS)

            for pc in range(NP):
                load(0, pc, before(0, pc, free0) if pc >= SLOTS else [], 0)
            with sp.Fori(1, NC) as c:
                for pc in range(NP):
                    load(c, pc, before(c, pc, free0), 0)
            for pc in range(NP):
                load(0, pc, before(0, pc, free1) if pc >= SLOTS else free0(NC - 1, pc + NP - SLOTS), 1)

            def store(c):
                sp.wait_ge(s_o, c + 1)
                sp.dma_start(out_v[:, c, :, :], o_st[:, :, :]).then_inc(s_out, 16)

            with sp.Fori(1, NC) as c:
                for pc in range(NP):
                    if pc == 6:
                        store(c - 1)
                    load(c, pc, before(c, pc, free1), 1)
            store(NC - 1)
            sp.wait_ge(s_out, 16 * NC)

            sp.wait_ge(s_flag, 1)
            with sp.If(sp.value_load(flag[0:1, 0:1], min_val=0, max_val=1) > 0):
                with sp.Fori(0, NC) as c:
                    for pc in range(NP):
                        sp.wait_ge(s_gma, NP * c + pc + 1)
                        sp.dma_start(ring[:, 0, :, :], adj_v[:, c, :, pc * PIECE:(pc + 1) * PIECE])\
                          .then_inc(s_gring, 16)
                    sp.wait_ge(s_go, c + 1)
                    sp.dma_start(out_v[:, c, :, :], o_st[:, :, :]).then_inc(s_out, 16)
                sp.wait_ge(s_out, 2 * 16 * NC)

        @block.gpsimd
        def _(pool):
            seq = [0]

            def link(ins):
                seq[0] += 1
                ins.then_inc(pool_seq, 1)
                pool.wait_ge(pool_seq, seq[0])

            nc.gpsimd.memset(ident[:, :], 0.0).then_inc(s_ident0, 1)
            pool.wait_ge(s_ident0, 1)
            nc.gpsimd.affine_select(out=ident[:, :], in_=ident[:, :], compare_op=ALU.not_equal, fill=1.0,
                                    base=0, pattern=[[-1, P]], channel_multiplier=1).then_inc(s_ident, 1)
            nc.gpsimd.memset(minus_one[:, :], -1.0)
            nc.gpsimd.memset(vals[:, :, 2 * D:2 * D + 1], H_SCALE).then_inc(s_ones, 1)

            def lo(c, p):
                n = nth(c, p)
                b = n_of(p) % NSPLIT
                pool.wait_ge(s_hi, n + 1)
                nc.gpsimd.tensor_tensor(split_lo[:, b, :], turned[:, n_of(p) % NTURN, :, :].rearrange("p j n -> p (j n)"),
                                        split_hi[:, b, :], ALU.subtract).then_inc(s_lo, 1)

            def scale_h0(m):
                pool.wait_ge(s_z0, m + 1)
                pool.wait_ge(s_rs0, m + 1)
                s8 = slice(8 * m, 8 * m + 8)
                nc.gpsimd.tensor_tensor(h0[:, s8, :], h0[:, s8, :], rs[:, s8].unsqueeze(2).broadcast_to([P, 8, D]),
                                        ALU.mult).then_inc(s_h0, 1)

            def stage_h(g):
                pool.wait_ge(s_h0, NGRP)
                nc.gpsimd.tensor_copy(h_st[:, :, :], h0[:, bass.ds(g * R, R), :]).then_inc(s_hst, 1)

            def gate(g, base):
                pool.wait_ge(s_nT, g + 1)
                nc.gpsimd.tensor_tensor(dT[:, :], hT[:, :], nT[:, :], ALU.subtract).then_inc(pool_seq, 1)
                pool.wait_ge(pool_seq, base + 1)
                nc.gpsimd.tensor_tensor(dT[:, :], dT[:, :], zT[:, :], ALU.mult).then_inc(pool_seq, 1)
                pool.wait_ge(pool_seq, base + 2)
                nc.gpsimd.tensor_tensor(dT[:, :], dT[:, :], nT[:, :], ALU.add).then_inc(s_g, 1)

            def h1(g):
                pool.wait_ge(s_rs, g + 1)
                nc.gpsimd.tensor_tensor(h1s[:, :, :], z1[:, :, :], h_scale[:, :].unsqueeze(2).broadcast_to([P, R, D]),
                                        ALU.mult).then_inc(s_h1, 1)
                nc.gpsimd.tensor_tensor(norm_t[:, :], va2[:, 0:R], rs2[:, 0:R], ALU.mult).then_inc(pool_norm, 1)
                pool.wait_ge(pool_norm, 2 * g + 1)
                nc.gpsimd.tensor_tensor(norm_inv[:, bass.ds(g * R, R)], norm_t[:, :], rs2[:, R:2 * R],
                                        ALU.mult).then_inc(pool_norm, 1)

            def vals_lo(g):
                pool.wait_ge(s_vh, g + 1)
                nc.gpsimd.tensor_tensor(vals[:, bass.ds(g * R, R), 0:D], h1s[:, :, :],
                                        vals[:, bass.ds(g * R, R), D:2 * D], ALU.subtract).then_inc(s_vl, 1)

            scale_h0(0)
            for p in ODD:
                lo(0, p)
                if p % 4 == 3 and p < NPAIR - 1:
                    scale_h0(p // 4 + 1)
            stage_h(0)

            def chunk0(c, older):
                for p in ODD:
                    if p == GATE:
                        gate(c - 1, 2 * (c - 1))
                    lo(c, p)
                    if older and p == 7:
                        h1(c - 2)
                    if p == 6:
                        stage_h(c)
                    if older and p == 11:
                        vals_lo(c - 2)

            chunk0(1, False)
            with pool.Fori(2, NC) as c:
                chunk0(c, True)
            def hold(i):
                nc.gpsimd.tensor_tensor(idle[:, i:i + 1], ident[:, 0:1], ident[:, 0:1], ALU.mult)

            def mask(c, pc):
                slot = pc % SLOTS
                if pc == 1:
                    pool.wait_ge(s_m, c + 1)
                pool.wait_ge(s_ring1[slot], 64 * (2 * c + 1 + pc // SLOTS))
                hold(pc)
                nc.gpsimd.tensor_scalar(ring[:, slot, :, :], ring[:, slot, :, :], -1.0, NEG * L_SCALE,
                                        ALU.add, ALU.mult).then_inc(pool_mask, 1)
                pool.wait_ge(pool_mask, NP // 2 * c + pc // 2 + 1)
                nc.gpsimd.tensor_tensor(ring_q[slot], ring_q[slot], m_now[:, :].unsqueeze(2)
                                        .broadcast_to([P, G, P]), ALU.subtract).then_inc(s_mq, 1)

            def output(c, first):
                pool.wait_ge(s_den, c + 1)
                nc.gpsimd.tensor_tensor(o_t[:, :, :], sums[:, :, 0:D], sums[:, :, D:2 * D], ALU.add).then_inc(pool_out, 1)
                pool.wait_ge(pool_out, 2 * c + 1)
                nc.gpsimd.tensor_tensor(o_t[:, :, :], o_t[:, :, :], o_den[:, :].unsqueeze(2).broadcast_to([P, R, D]),
                                        ALU.mult).then_inc(pool_out, 1)
                pool.wait_ge(pool_out, 2 * c + 2)
                if not first:
                    pool.wait_ge(s_out, 16 * c)
                hold(NP)
                nc.gpsimd.tensor_tensor(o_st[:, :, :], o_t[:, :, :], xs[:, bass.ds(c * R, R), :], ALU.add).then_inc(s_o, 1)

            h1(NC - 2)
            mask(0, 1)
            vals_lo(NC - 2)
            mask(0, 3)
            h1(NC - 1)
            mask(0, 5)
            vals_lo(NC - 1)
            mask(0, 7)

            def chunk1(c, first):
                for pc in (1, 3, 5, 7):
                    if pc == 5:
                        output(c - 1, first)
                    mask(c, pc)

            chunk1(1, True)
            with pool.Fori(2, NC) as c:
                chunk1(c, False)

        @block.scalar
        def _(act):
            for part, (b0, b1) in enumerate(((0, 2), (2, 4), (4, NC))):
                act.dma_start(xs[:, R * b0:R * b1, :].rearrange("p (b j) d -> p b (j d)", j=R),
                              x_v[:, b0:b1, :]).then_inc(s_x[part], 16)
            act.dma_start(w_nat[:, 0, :], W_msg).then_inc(s_w, 16)
            act.dma_start(w_nat[:, 1:4, :], W_ih.rearrange("(g e) d -> e g d", g=3)).then_inc(s_w, 16)
            act.dma_start(w_nat[:, 4:7, :], W_hh.rearrange("(g e) d -> e g d", g=3)).then_inc(s_w, 16)
            act.dma_start(b_m[:, :], b_msg.rearrange("(e a) -> e a", a=1)).then_inc(s_b, 16)
            act.dma_start(b_i[:, :], b_ih.rearrange("(g e) -> e g", g=3),
                          allow_slow_non_contiguous=True).then_inc(s_b, 16)
            act.dma_start(b_h[:, :], b_hh.rearrange("(g e) -> e g", g=3),
                          allow_slow_non_contiguous=True).then_inc(s_b, 16)
            act.dma_start(bt[:, :], beta.partition_broadcast(P)).then_inc(s_b, 16)

            def take_weights():
                act.wait_ge(s_wps, 1)
                nc.scalar.activation(wT[:, 0:4, :], ps[:, 6, :].rearrange("p (g n) -> p g n", g=4),
                                     ACT.Copy).then_inc(s_wsb, 1)
                nc.scalar.activation(wT[:, 4:7, :], ps[:, 7, 0:3 * P].rearrange("p (g n) -> p g n", g=3),
                                     ACT.Copy).then_inc(s_wsb, 1)

            def h_z(m):
                act.wait_ge(s_st, m + 1)
                for t in range(8 * m, 8 * m + 8):
                    last = nc.scalar.activation(h0[:, t, :], xs[:, t, :], ACT.Relu, bias=neg_mean[:, t:t + 1])
                last.then_inc(s_z0, 1)

            def h_hi(m):
                act.wait_ge(s_h0, m + 1)
                nc.scalar.activation(h0_hi[:, 4 * m:4 * m + 4, :], h0[:, 8 * m + 4:8 * m + 8, :], ACT.Copy,
                                     scale=H_SCALE).then_inc(s_h0hi, 1)

            def evacuate(c, p):
                n = nth(c, p)
                if even(p):
                    b = n_of(p) % NWHOLE
                    act.wait_ge(s_t, n + 1)
                    if p >= 4 or not (isinstance(c, int) and c == 0):
                        act.wait_ge(s_agg, NPAIR * c + p - 3)
                    nc.scalar.activation(whole[:, b, :], tile2[p % 2], ACT.Copy,
                                         scale=A_SCALE * H_SCALE).then_inc(s_w32, 1)
                else:
                    t, b = n_of(p) % NTURN, n_of(p) % NSPLIT
                    pair = turned[:, t, :, :].rearrange("p j n -> p (j n)")
                    act.wait_ge(s_tn, n + 1)
                    nc.scalar.activation(pair, pair, ACT.Copy, scale=A_SCALE).then_inc(s_ts, 1)
                    act.wait_ge(s_ts, n + 1)
                    if p >= 10 or not (isinstance(c, int) and c == 0):
                        act.wait_ge(s_agg, NPAIR * c + p - 7)
                    nc.scalar.activation(split_hi[:, b, :], pair, ACT.Copy).then_inc(s_hi, 1)

            def take_agg(g):
                act.wait_ge(s_agg, NPAIR * (g + 1))
                nc.scalar.activation(aggT[:, :], AGG, ACT.Copy, scale=1.0 / (H_SCALE * A_SCALE)).then_inc(s_aggT, 1)

            def take_qk(g, bank=G6):
                act.wait_ge(s_qps, g + 1)
                nc.scalar.activation(q_hi[:, bass.ds(g * CH, CH)], bank, ACT.Copy, scale=Q_SCALE)
                nc.scalar.activation(k_hi[:, bass.ds(g * CH, CH)], bank, ACT.Copy,
                                     scale=k_scale[:, :]).then_inc(s_qk, 1)

            def gru(g, p, msg=G7):
                if p == 4:
                    act.wait_ge(s_hTps, g + 1)
                    nc.scalar.activation(hT[:, :], G5, ACT.Copy).then_inc(s_hT, 1)
                    act.wait_ge(s_mps, g + 1)
                    nc.scalar.activation(msgT[:, :], msg, ACT.Relu, bias=b_m[:, :]).then_inc(s_msg, 1)
                if p == 8:
                    act.wait_ge(s_rzps, g + 1)
                    nc.scalar.activation(rT[:, :], G7, ACT.Sigmoid, bias=b_rz[:, 0:1])
                    nc.scalar.activation(zT[:, :], G5, ACT.Sigmoid, bias=b_rz[:, 1:2]).then_inc(s_rz, 1)
                if p == 11:
                    act.wait_ge(s_tT, g + 1)
                    nc.scalar.activation(nT[:, :], tT[:, :], ACT.Tanh, bias=b_i[:, 2:3]).then_inc(s_nT, 1)

            def late(g, p):
                if p == 2:
                    act.wait_ge(s_z1, g + 1)
                    for r in range(R):
                        last = nc.scalar.activation(sq[:, r, :], z1[:, r, :], ACT.Square, accum_out=n2[:, r:r + 1])
                    last.then_inc(s_n2, 1)
                if p == 7:
                    take_qk(g)
                if p == 9:
                    act.wait_ge(s_h1, g + 1)
                    nc.scalar.activation(vals[:, bass.ds(g * R, R), D:2 * D], h1s[:, :, :], ACT.Copy).then_inc(s_vh, 1)

            h_z(0)
            for p in range(NPAIR):
                evacuate(0, p)
                if p == 1:
                    h_hi(0)
                if p % 4 == 3 and p < NPAIR - 1:
                    h_z(p // 4 + 1)
                if p % 4 == 0 and p:
                    h_hi(p // 4)
                if p == 12:
                    take_weights()
            evacuate(1, 0)
            evacuate(1, 2)
            act.wait_ge(s_bias, 1)
            take_agg(0)
            evacuate(1, 1)

            def chunk0(c, older, final):
                if older:
                    late(c - 2, 2)
                for p in range(3, NPAIR):
                    evacuate(c, p)
                    gru(c - 1, p)
                    if older:
                        late(c - 2, p)
                if not final:
                    evacuate(c + 1, 0)
                    evacuate(c + 1, 2)
                take_agg(c)
                if not final:
                    evacuate(c + 1, 1)

            chunk0(1, False, False)
            with act.Fori(2, NC - 1) as c:
                chunk0(c, True, False)
            chunk0(NC - 1, True, True)

            def less_one(c, m, r):
                pc = 2 * m
                if r == 0:
                    act.wait_ge(s_ring1[pc % SLOTS], 16 * (2 * c + 1 + pc // SLOTS))
                nc.scalar.activation(masks[:, m % 2, r, :], ring[:, pc % SLOTS, r, :], ACT.Identity,
                                     bias=minus_one[:, :]).then_inc(s_ma, 1)

            gru(NC - 1, 4, ps[:, 0, :])
            late(NC - 2, 2)
            less_one(0, 0, 0)
            less_one(0, 0, 1)
            gru(NC - 1, 8)
            less_one(0, 0, 2)
            less_one(0, 0, 3)
            gru(NC - 1, 11)
            late(NC - 2, 7)
            late(NC - 2, 9)
            for r in range(R):
                less_one(0, 1, r)
            def probs(c, n):
                U = NK * c + n
                if tile_of(n)[2]:
                    act.wait_ge(s_am, NK // 2 * c + n // 2 + 1)
                else:
                    act.wait_ge(s_s, U + 1)
                if not (isinstance(c, int) and U < NB):
                    act.wait_ge(s_pv, U - NB + 1)
                nc.scalar.activation(p_hi[:, n % NB, :], ps[:, n % NB, :], ACT.Exp,
                                     bias=p_bias[:, :], scale=1.0 / L_SCALE)
                nc.scalar.activation(ps[:, n % NB, :], ps[:, n % NB, :], ACT.Exp,
                                     bias=p_bias[:, :], scale=1.0 / L_SCALE).then_inc(s_p, 1)

            def take_sums(c, first):
                act.wait_ge(s_pv, NK * (c + 1))
                if not first:
                    act.wait_ge(s_o, c)
                for r in (2, 3):
                    nc.scalar.activation(sums[:, r, :], accs[r][:, 0:W], ACT.Copy).then_inc(s_acca, 1)

            def chunk1(c, age, final):
                for n in range(NK):
                    if age and n == 2:
                        take_sums(c - 1, age == 1)
                    if age or n:
                        probs(c, n)
                    if age == 0 and n == 7:
                        take_qk(NC - 1, ps[:, 0, :])
                    if age == 0:
                        late(NC - 1, n if n == 9 else 0)
                    m = (n + 2) // 8 + 1
                    if n % 8 in LESS_AT and (m < NGRP or not final) and not (n < 6 and age == 0):
                        less_one(*((c, m) if m < NGRP else (c + 1, m - NGRP)), LESS_AT.index(n % 8))

            probs(0, 0)
            late(NC - 1, 2)
            chunk1(0, 0, False)
            chunk1(1, 1, False)
            with act.Fori(2, NC - 1) as c:
                chunk1(c, 2, False)
            chunk1(NC - 1, 2, True)
            take_sums(NC - 1, False)

            act.wait_ge(s_flag, 1)
            with act.If(act.value_load(flag[0:1, 0:1], min_val=0, max_val=1) > 0):
                with act.Fori(0, NC) as c:
                    for n in range(NK):
                        act.wait_ge(s_gl, NK * c + n + 1)
                        nc.scalar.activation(p_hi[:, 0, :], ps[:, 0, :], ACT.Exp, bias=p_bias[:, :], scale=1.0 / L_SCALE)
                        nc.scalar.activation(ps[:, 0, :], ps[:, 0, :], ACT.Exp, bias=p_bias[:, :],
                                             scale=1.0 / L_SCALE).then_inc(s_gp, 1)

        @block.vector
        def _(dve):
            seq = [0]

            def link(ins):
                seq[0] += 1
                ins.then_inc(dve_seq, 1)
                dve.wait_ge(dve_seq, seq[0])

            def rsqrt(y, a, t, h, chain):
                chain(nc.vector.tensor_scalar(y.bitcast(i32), a.bitcast(i32), -0.5, float(0x5F3759DF), ALU.mult, ALU.add))
                chain(nc.vector.tensor_scalar(h, a, -0.5, None, ALU.mult))
                for _ in range(3):
                    chain(nc.vector.tensor_tensor(t, y, y, ALU.mult))
                    chain(nc.vector.tensor_tensor(t, t, h, ALU.mult))
                    chain(nc.vector.scalar_tensor_tensor(out=y, in0=t, scalar=1.5, in1=y, op0=ALU.add, op1=ALU.mult))

            def statistics(t0, t1):
                dve.wait_ge(s_x[min(t0 // 8, 2)], 16)
                for t in range(t0, t1):
                    last = nc.vector.bn_stats(stats[:, t, :], xs[:, t, :])
                link(last)
                for t in range(t0, t1):
                    last = nc.vector.bn_aggr(mv[:, t, :], stats[:, t, :])
                link(last)
                s8 = slice(t0, t1)
                nc.vector.tensor_scalar(neg_mean[:, s8], mv[:, s8, 0], -1.0, None, ALU.mult).then_inc(s_st, 1)
                link(nc.vector.tensor_scalar(va[:, s8], mv[:, s8, 1], LN_EPS, None, ALU.add))
                rsqrt(rs[:, s8], va[:, s8], nt1[:, s8], nt2[:, s8], link)
                nc.vector.tensor_scalar(rs[:, s8], rs[:, s8], 1.0, None, ALU.mult).then_inc(s_rs0, 1)

            def h_lo(m):
                dve.wait_ge(s_h0hi, m + 1)
                nc.vector.scalar_tensor_tensor(out=h0_lo[:, 4 * m:4 * m + 4, :], in0=h0[:, 8 * m + 4:8 * m + 8, :],
                                               scalar=H_SCALE, in1=h0_hi[:, 4 * m:4 * m + 4, :],
                                               op0=ALU.mult, op1=ALU.subtract).then_inc(s_h0lo, 1)

            def turn(c, p):
                n, pc, j0 = nth(c, p), p // 2, 2 * (p % 2)
                if p % 2 == 0:
                    dve.wait_ge(s_ring[pc % SLOTS], 64 * (2 * c + 1 + pc // SLOTS))
                if p >= 6 or not (isinstance(c, int) and c == 0):
                    dve.wait_ge(s_lo, n - NTURN + 1)
                nc.vector.transpose(turned[:, n_of(p) % NTURN, :, :],
                                    ring_q[pc % SLOTS].rearrange("p g (c j) -> p j g c", c=QD)
                                    [:, j0:j0 + 2, :, :]).then_inc(s_tn, 1)

            def row_max(c, pc):
                if pc % 2 == 0:
                    dve.wait_ge(s_t, nth(c, 2 * pc + 1) + 1)
                    nc.vector.tensor_reduce(mx[:, pc // 2, bass.ds(c, 1), :].rearrange("p a r -> p (a r)"),
                                            ring[:, pc % SLOTS, :, :], AX.X, ALU.max).then_inc(s_mxd, 1)
                else:
                    nc.vector.tensor_reduce(mxq[:, pc // 2, bass.ds(c * G, G)], ring_q[pc % SLOTS], AX.X,
                                            ALU.max).then_inc(s_mxd, 1)

            LINKS, NORM_LINKS = 3, 12

            def gru(g, stage, bank=G6, n_h=G6, n_i=G7):
                done = [1 if stage == "x1" else 0]

                def link_g(ins):
                    done[0] += 1
                    ins.then_inc(dve_gru, 1)
                    dve.wait_ge(dve_gru, LINKS * g + done[0])

                def link_n(ins):
                    done[0] += 1
                    ins.then_inc(dve_norm, 1)
                    dve.wait_ge(dve_norm, NORM_LINKS * g + done[0])

                if stage == "t":
                    dve.wait_ge(s_nps, g + 1)
                    link_g(nc.vector.scalar_tensor_tensor(out=tT[:, :], in0=n_h, scalar=b_h[:, 2:3], in1=rT[:, :],
                                                          op0=ALU.add, op1=ALU.mult))
                    nc.vector.tensor_tensor(tT[:, :], n_i, tT[:, :], ALU.add).then_inc(s_tT, 1)
                if stage == "x1":
                    x1 = xs[:, bass.ds(g * R, R), :]
                    dve.wait_ge(s_gps, g + 1)
                    nc.vector.tensor_tensor(x1_st[:, :, :], G5.rearrange("p (r d) -> p r d", r=R), x1,
                                            ALU.add).then_inc(s_x1, 1)
                    dve.wait_ge(s_x1, g + 1)
                    nc.vector.tensor_scalar(xs[:, bass.ds(g * R, 2), :], x1_st[:, 0:2, :], 1.0, None, ALU.mult)
                    for r in range(R):
                        last = nc.vector.bn_stats(stats[:, r, :], x1_st[:, r, :])
                    link_g(last)
                    nc.vector.tensor_scalar(xs[:, bass.ds(g * R + 2, 2), :], x1_st[:, 2:4, :], 1.0, None, ALU.mult)
                    for r in range(R):
                        last = nc.vector.bn_aggr(mv[:, r, :], stats[:, r, :])
                    link_g(last)
                    if not (isinstance(g, int) and g == 0):
                        dve.wait_ge(pool_norm, 2 * g)
                    for r in range(R):
                        last = nc.vector.tensor_scalar(z1[:, r, :], x1_st[:, r, :], mv[:, r, 0:1], 0.0,
                                                       ALU.subtract, ALU.max)
                    last.then_inc(s_z1, 1)
                    nc.vector.tensor_scalar(va2[:, 0:R], mv[:, 0:R, 1], LN_EPS, None, ALU.add)
                if stage == "norm":
                    dve.wait_ge(s_n2, g + 1)
                    link_n(nc.vector.tensor_scalar(va2[:, R:2 * R], n2[:, :], 1e-30, None, ALU.max))
                    rsqrt(rs2[:, :], va2[:, :], c1[:, :], c2[:, :], link_n)
                    nc.vector.tensor_scalar(h_scale[:, :], rs2[:, 0:R], H_SCALE, None, ALU.mult).then_inc(s_rs, 1)
                    for r in range(R):
                        last = nc.vector.tensor_scalar(h1n[:, r, :], z1[:, r, :], rs2[:, R + r:R + r + 1], None,
                                                       ALU.mult)
                    last.then_inc(s_h1n, 1)
                if stage == "qk":
                    dve.wait_ge(s_qk, g + 1)
                    cols = bass.ds(g * CH, CH)
                    nc.vector.scalar_tensor_tensor(out=q_lo[:, cols], in0=bank, scalar=Q_SCALE, in1=q_hi[:, cols],
                                                   op0=ALU.mult, op1=ALU.subtract)
                    nc.vector.scalar_tensor_tensor(out=k_lo[:, cols], in0=bank, scalar=k_scale[:, :], in1=k_hi[:, cols],
                                                   op0=ALU.mult, op1=ALU.subtract).then_inc(s_qkl, 1)

            statistics(0, 8)
            statistics(8, 16)
            turn(0, 2)
            turn(0, 3)
            h_lo(0)
            row_max(0, 0)
            row_max(0, 1)
            for m in range(1, NGRP):
                turn(0, 4 * m + 2)
                row_max(0, 2 * m)
                turn(0, 4 * m + 3)
                h_lo(m)
                if m < NGRP - 1:
                    statistics(8 * m + 8, 8 * m + 16)
                row_max(0, 2 * m + 1)
            turn(1, 2)
            dve.wait_ge(s_b, 64)
            nc.vector.tensor_tensor(b_rz[:, :], b_i[:, 0:2], b_h[:, 0:2], ALU.add)
            nc.vector.tensor_scalar(k_scale[:, :], bt[:, :], Q_SCALE, None, ALU.mult)
            link(nc.vector.tensor_scalar(bt_neg[:, :], bt[:, :], -1.0, None, ALU.mult))
            link(nc.vector.tensor_tensor(p_bias[:, :], bt[:, :], bt_neg[:, :], ALU.max))
            nc.vector.tensor_scalar(p_bias[:, :], p_bias[:, :], -1.0, P_LOG_SCALE, ALU.mult, ALU.add).then_inc(s_bias, 1)

            def chunk0(c, older, final):
                turn(c, 3)
                row_max(c, 0)
                row_max(c, 1)
                turn(c, 6)
                if older:
                    gru(c - 2, "norm")
                row_max(c, 2)
                turn(c, 7)
                row_max(c, 3)
                turn(c, 10)
                row_max(c, 4)
                if older:
                    gru(c - 2, "qk")
                turn(c, 11)
                gru(c - 1, "t")
                row_max(c, 5)
                turn(c, 14)
                row_max(c, 6)
                turn(c, 15)
                row_max(c, 7)
                if not final:
                    turn(c + 1, 2)
                gru(c - 1, "x1")

            chunk0(1, False, False)
            with dve.Fori(2, NC - 1) as c:
                chunk0(c, True, False)
            chunk0(NC - 1, True, True)

            dve.wait_ge(s_mxd, NP * NC)
            link(nc.vector.tensor_reduce(mxo[:, :], mxq[:, :, :].rearrange("p h t -> p t h"), AX.X, ALU.max))
            mo = mxo[:, :].rearrange("p (c r q) -> p c r q", c=NC, r=R)
            for a in range(4):
                for q in range(4):
                    last = nc.vector.tensor_scalar(mx[QD * q:QD * (q + 1), 4 + a, :, :],
                                                   mo[QD * a:QD * (a + 1), :, :, q], 1.0, None, ALU.mult)
            link(last)
            gru(NC - 2, "norm")
            dve.wait_ge(s_rz, NC)
            gru(NC - 1, "t", n_h=ps[:, 3, :], n_i=ps[:, 2, :])
            link(nc.vector.tensor_reduce(m_row[:, :], mx[:, :, :, :].rearrange("p h c r -> p (c r) h"), AX.X, ALU.max))
            link(nc.vector.tensor_scalar(m_row[:, :], m_row[:, :], -1.0, NEG * L_SCALE, ALU.add, ALU.mult))
            mr = m_row[:, :].rearrange("p (c r) -> p c r", c=NC)
            for a in range(4):
                for q in range(4):
                    last = nc.vector.tensor_scalar(m_quad[QD * a:QD * (a + 1), :, q::4],
                                                   mr[QD * q:QD * (q + 1), :, :], 1.0, None, ALU.mult)
            link(last)
            nc.vector.tensor_scalar(m_now[:, :], m_quad[:, 0, :], 1.0, None, ALU.mult).then_inc(s_m, 1)

            def scale_mask(c, m, r):
                dve.wait_ge(s_ma, NK // 2 * c + KB * m + r + 1)
                last = nc.vector.tensor_scalar(masks[:, m % 2, r, :], masks[:, m % 2, r, :], NEG * L_SCALE,
                                               m_row[:, bass.ds(c * R + r, 1)], ALU.mult, ALU.subtract)
                if r == R - 1:
                    last.then_inc(s_mk, 1)

            dve.wait_ge(s_nT, NC)
            link(nc.vector.tensor_tensor(dT[:, :], hT[:, :], nT[:, :], ALU.subtract))
            link(nc.vector.tensor_tensor(dT[:, :], dT[:, :], zT[:, :], ALU.mult))
            nc.vector.tensor_tensor(dT[:, :], dT[:, :], nT[:, :], ALU.add).then_inc(s_g, 1)
            for r in range(R):
                scale_mask(0, 0, r)
            gru(NC - 1, "x1")
            gru(NC - 2, "qk")

            def turn_mask(c, i):
                slot, j = (i // KB * 2 + 1) % SLOTS, i % KB
                if j == 0:
                    dve.wait_ge(s_mq, NP // 2 * c + i // KB + 1)
                nc.vector.transpose(turned_mask[:, i % 4, :],
                                    ring_q[slot].rearrange("p g (c j) -> p j g c", c=QD)[:, j, :, :]).then_inc(s_tm, 1)

            def add_mask(c, i):
                bank = ps[:, (2 * i + 1) % NB, :]
                dve.wait_ge(s_s, NK * c + 2 * i + 2)
                dve.wait_ge(s_tm, NK // 2 * c + i + 1)
                nc.vector.tensor_tensor(bank, bank, turned_mask[:, i % 4, :], ALU.add).then_inc(s_am, 1)

            def probs_lo(c, n):
                dve.wait_ge(s_p, NK * c + n + 1)
                nc.vector.tensor_tensor(p_lo[:, n % NB, :], ps[:, n % NB, :], p_hi[:, n % NB, :],
                                        ALU.subtract).then_inc(s_pl, 1)

            def take_sums(c, first):
                dve.wait_ge(s_pv, NK * (c + 1))
                if not first:
                    dve.wait_ge(s_o, c)
                for r in (0, 1):
                    nc.vector.tensor_scalar(sums[:, r, :], accs[r][:, 0:W], 1.0, None, ALU.mult).then_inc(s_accd, 1)

            def invert(c):
                dve.wait_ge(s_accd, 2 * (c + 1))
                dve.wait_ge(s_acca, 2 * (c + 1))
                nc.vector.reciprocal(o_den[:, :], sums[:, :, 2 * D]).then_inc(s_den, 1)

            def chunk1(c, age, final):
                for n in range(NK):
                    i = n // 2 + 1
                    if n % 2 and (i < NK // 2 or not final):
                        add_mask(*((c, i) if i < NK // 2 else (c + 1, i - NK // 2)))
                    if n + 1 < NK or not final:
                        probs_lo(*((c, n + 1) if n + 1 < NK else (c + 1, 0)))
                    i += 2
                    if n % 2 and (i < NK // 2 or not final):
                        turn_mask(*((c, i) if i < NK // 2 else (c + 1, i - NK // 2)))
                    m = (n + 2) // 8 + 1
                    if n % 8 in SCALE_AT and (m < NGRP or not final) and not (n < 6 and age == 0):
                        scale_mask(*((c, m) if m < NGRP else (c + 1, m - NGRP)), SCALE_AT.index(n % 8))
                    if n == 19 and not final:
                        nc.vector.tensor_scalar(m_now[:, :], m_quad[:, bass.ds(c + 1, 1), :].rearrange("p a m -> p (a m)"),
                                                1.0, None, ALU.mult).then_inc(s_m, 1)
                    if age and n == 1:
                        invert(c - 1)
                    if age == 0 and n == 6:
                        gru(NC - 1, "qk", ps[:, 0, :])
                    if age == 0 and n == 22:
                        choose_path()
                take_sums(c, age == 0)

            def choose_path():
                dve.wait_ge(pool_norm, 2 * NC)
                link(nc.vector.memset(worst[:, :], 0.0))
                link(nc.vector.tensor_reduce(worst[:, 0:1], norm_inv[:, :], AX.X, ALU.max))
                link(nc.vector.transpose(worst_t[:, :], worst[:, :]))
                link(nc.vector.tensor_reduce(worst[:, 0:1], worst_t[:, :], AX.X, ALU.max))
                for a in range(4):
                    last = nc.vector.tensor_scalar(worst_t[0:1, a:a + 1], worst[QD * a:QD * a + 1, 0:1], 1.0, None,
                                                   ALU.mult)
                link(last)
                link(nc.vector.tensor_reduce(worst[0:1, 0:1], worst_t[0:1, 0:4], AX.X, ALU.max))
                nc.vector.tensor_scalar(flag[0:1, :], worst[0:1, 0:1], NORM_INV_MAX, None, ALU.is_gt).then_inc(s_flag, 1)

            for i in range(3):
                turn_mask(0, i)
            add_mask(0, 0)
            probs_lo(0, 0)
            gru(NC - 1, "norm")
            for r in range(R):
                scale_mask(0, 1, r)
            chunk1(0, 0, False)
            with dve.Fori(1, NC - 1) as c:
                chunk1(c, 1, False)
            chunk1(NC - 1, 1, True)
            invert(NC - 1)
            dve.wait_ge(s_den, NC)
            dve.wait_ge(s_o, NC - 1)
            link(nc.vector.tensor_tensor(o_t[:, :, :], sums[:, :, 0:D], sums[:, :, D:2 * D], ALU.add))
            link(nc.vector.tensor_tensor(o_t[:, :, :], o_t[:, :, :], o_den[:, :].unsqueeze(2).broadcast_to([P, R, D]),
                                         ALU.mult))
            dve.wait_ge(s_out, 16 * (NC - 1))
            nc.vector.tensor_tensor(o_st[:, :, :], o_t[:, :, :], xs[:, R * (NC - 1):R * NC, :], ALU.add).then_inc(s_o, 1)

            diag, ones, a_row, fac = (t[:, :] for t in (hT, rT, msgT, tT))
            diag = diag.rearrange("p (r n) -> p r n", r=R)
            GEN_LINKS = NP + 3 * NK + 5

            def general(c):
                done = [0]

                def link_c(ins):
                    done[0] += 1
                    ins.then_inc(dve_gen, 1)
                    dve.wait_ge(dve_gen, GEN_LINKS * c + done[0] + 2)

                for r in range(R):
                    last = nc.vector.tensor_scalar(diag[:, r, :], ident[:, :], norm_inv[:, bass.ds(c * R + r, 1)], None,
                                                   ALU.mult)
                last.then_inc(s_gdiag, 1)
                dve.wait_ge(s_gbc, c + 1)
                link_c(nc.vector.tensor_scalar(a_row, ps[:, 2, :], EPS, None, ALU.mult))
                for pc in range(NP):
                    dve.wait_ge(s_gring, 16 * (NP * c + pc + 1))
                    link_c(nc.vector.tensor_scalar(masks[:, 0, :, :], ring[:, 0, :, :], -1.0, NEG * L_SCALE,
                                                   ALU.add, ALU.mult))
                    for r in range(R):
                        last = nc.vector.tensor_scalar(masks[:, 0, r, :], masks[:, 0, r, :],
                                                       m_row[:, bass.ds(c * R + r, 1)], None, ALU.subtract)
                        if r == 0:
                            last.then_inc(s_gma, 1)
                    last.then_inc(s_gmk, 1)
                    for j in range(KB):
                        n = KB * pc + j
                        dve.wait_ge(s_gs, NK * c + n + 1)
                        link_c(nc.vector.tensor_scalar(fac, a_row, norm_inv[:, n:n + 1], 1.0, ALU.mult, ALU.add))
                        link_c(nc.vector.reciprocal(fac, fac))
                        link_c(nc.vector.tensor_tensor(fac, ps[:, 1, :], fac, ALU.mult))
                        nc.vector.tensor_tensor(ps[:, 0, :], ps[:, 0, :], fac, ALU.add).then_inc(s_gl, 1)
                        dve.wait_ge(s_gp, NK * c + n + 1)
                        nc.vector.tensor_tensor(p_lo[:, 0, :], ps[:, 0, :], p_hi[:, 0, :], ALU.subtract).then_inc(s_gpl, 1)
                dve.wait_ge(s_gpv, NK * (c + 1))
                for r in range(R):
                    last = nc.vector.tensor_scalar(sums[:, r, :], accs[r][:, 0:W], 1.0, None, ALU.mult)
                link_c(last)
                nc.vector.tensor_scalar(idle_v[:, :], minus_one[:, :], 1.0, None, ALU.mult).then_inc(s_gacc, 1)
                link_c(nc.vector.reciprocal(o_den[:, :], sums[:, :, 2 * D]))
                link_c(nc.vector.tensor_tensor(o_t[:, :, :], sums[:, :, 0:D], sums[:, :, D:2 * D], ALU.add))
                for r in range(R):
                    last = nc.vector.tensor_scalar(o_t[:, r, :], o_t[:, r, :], o_den[:, r:r + 1], None, ALU.mult)
                link_c(last)
                dve.wait_ge(s_out, 16 * (NC + c))
                nc.vector.tensor_tensor(o_st[:, :, :], o_t[:, :, :], xs[:, bass.ds(c * R, R), :], ALU.add).then_inc(s_go, 1)
                assert done[0] == GEN_LINKS, done

            dve.wait_ge(s_flag, 1)
            with dve.If(dve.value_load(flag[0:1, 0:1], min_val=0, max_val=1) > 0):
                dve.wait_ge(s_o, NC)
                nc.vector.memset(ones, 1.0).then_inc(dve_gen, 1)
                dve.wait_ge(dve_gen, 1)
                nc.vector.tensor_scalar(idle_v[:, :], minus_one[:, :], 1.0, None, ALU.mult).then_inc(s_gacc, 1)
                nc.vector.tensor_scalar(fac[:, 0:1], minus_one[:, :], 1.0, None, ALU.mult).then_inc(s_gma, 1)
                nc.vector.tensor_scalar(fac[:, 1:2], minus_one[:, :], 1.0, None, ALU.mult).then_inc(dve_gen, 1)
                dve.wait_ge(dve_gen, 2)
                with dve.Fori(0, NC) as c:
                    general(c)

        @block.tensor
        def _(pe):
            def block_T(dst, src, first=True):
                return nc.tensor.matmul(dst, lhsT=src, rhs=ident[:, :], start=first, stop=True,
                                        is_transpose=True, skip_group_check=True)

            def transpose_weights():
                pe.wait_ge(s_w, 48)
                for i in range(7):
                    last = block_T(ps[:, 6 + i // 4, (i % 4) * P:(i % 4 + 1) * P], w_nat[:, i, :])
                last.then_inc(s_wps, 1)

            def transposes(c, p):
                n, pc = nth(c, p), p // 2
                if p % 2 == 0:
                    pe.wait_ge(s_ring[pc % SLOTS], 16 * (2 * c + 1 + pc // SLOTS))
                if p >= 4 or not (isinstance(c, int) and c == 0):
                    pe.wait_ge(s_w32, n - 1)
                for b in range(2):
                    for r in range(R):
                        last = block_T(tile2[p % 2][:, b * CH + r * P:b * CH + (r + 1) * P],
                                       tile_cols(ring[:, pc % SLOTS, r, :], 2 * (p % 2) + b))
                last.then_inc(s_t, 1)

            def aggregate(c, p):
                n, first_chunk = nth(c, p), isinstance(c, int) and c == 0
                if first_chunk and p % 2 == 0:
                    pe.wait_ge(s_h0 if even(p) else s_h0lo, p // 4 + 1)
                pe.wait_ge(s_w32 if even(p) else s_lo, n + 1)
                if p == 0 and not first_chunk:
                    pe.wait_ge(s_aggT, c)
                for b in range(2):
                    k, cols = 2 * p + b, slice(b * CH, (b + 1) * CH)
                    first, final = k == 0, k == NK - 1
                    if even(p):
                        last = nc.tensor.matmul(AGG, lhsT=h0[:, k, :], rhs=whole[:, n_of(p) % NWHOLE, cols],
                                                start=first, stop=final)
                    else:
                        ah, al = split_hi[:, n_of(p) % NSPLIT, cols], split_lo[:, n_of(p) % NSPLIT, cols]
                        ko = KB * (p // 4) + k % KB
                        nc.tensor.matmul(AGG, lhsT=h0_hi[:, ko, :], rhs=ah, start=first, stop=False)
                        nc.tensor.matmul(AGG, lhsT=h0_hi[:, ko, :], rhs=al, start=False, stop=False)
                        last = nc.tensor.matmul(AGG, lhsT=h0_lo[:, ko, :], rhs=ah, start=False, stop=final)
                last.then_inc(s_agg, 1)

            def gru(g, p, older=True):
                if p == 1:
                    pe.wait_ge(s_hst, g + 1)
                    if older:
                        pe.wait_ge(s_x1, g)
                    for r in range(R):
                        last = block_T(tile_cols(G5, r), h_st[:, r, :])
                    last.then_inc(s_hTps, 1)
                if p == 2:
                    pe.wait_ge(s_aggT, g + 1)
                    nc.tensor.matmul(G7, lhsT=wT[:, 0, :], rhs=aggT[:, :], start=True, stop=True).then_inc(s_mps, 1)
                if p == 5:
                    pe.wait_ge(s_msg, g + 1)
                    for gate, dst in ((0, G7), (1, G5)):
                        nc.tensor.matmul(dst, lhsT=wT[:, 1 + gate, :], rhs=msgT[:, :], start=True, stop=False)
                        last = nc.tensor.matmul(dst, lhsT=wT[:, 4 + gate, :], rhs=hT[:, :], start=False, stop=True)
                    last.then_inc(s_rzps, 1)
                if p == 8:
                    pe.wait_ge(s_rz, g + 1)
                    if older:
                        pe.wait_ge(s_qkl, g)
                    nc.tensor.matmul(G6, lhsT=wT[:, 6, :], rhs=hT[:, :], start=True, stop=True)
                    nc.tensor.matmul(G7, lhsT=wT[:, 3, :], rhs=msgT[:, :], start=True, stop=True).then_inc(s_nps, 1)
                if p == GATE_T:
                    pe.wait_ge(s_g, g + 1)
                    for r in range(R):
                        last = block_T(G5[:, r * P:(r + 1) * P], tile_cols(dT[:, :], r))
                    last.then_inc(s_gps, 1)

            def normalised(g, bank):
                pe.wait_ge(s_h1n, g + 1)
                for r in range(R):
                    last = block_T(tile_cols(bank, r), h1n[:, r, :])
                last.then_inc(s_qps, 1)

            def chunk0(c, age, final):
                for p in range(NPAIR):
                    if even((p + 3) % NPAIR) and p < NPAIR - 3:
                        transposes(c, p + 3)
                    if p == NPAIR - 3 and not final:
                        transposes(c + 1, 0)
                    aggregate(c, p)
                    if age == 0 and p == 4:
                        transpose_weights()
                    if age >= 1:
                        gru(c - 1, p, older=age >= 2)
                    if age >= 2 and p == 4:
                        normalised(c - 2, G6)
                if not final:
                    transposes(c + 1, 1)

            pe.wait_ge(s_ident, 1)
            transposes(0, 0)
            transposes(0, 1)
            chunk0(0, 0, False)
            pe.wait_ge(s_wsb, 2)
            chunk0(1, 1, False)
            with pe.Fori(2, NC - 1) as c:
                chunk0(c, 2, False)
            chunk0(NC - 1, 2, True)
            gru(NC - 1, 1)
            pe.wait_ge(s_aggT, NC)
            pe.wait_ge(s_w32, NC * NPAIR // 2)
            nc.tensor.matmul(ps[:, 0, :], lhsT=wT[:, 0, :], rhs=aggT[:, :], start=True, stop=True).then_inc(s_mps, 1)
            pe.wait_ge(s_hT, NC)
            nc.tensor.matmul(G7, lhsT=wT[:, 4, :], rhs=hT[:, :], start=True, stop=False)
            nc.tensor.matmul(G5, lhsT=wT[:, 5, :], rhs=hT[:, :], start=True, stop=False)
            pe.wait_ge(s_msg, NC)
            nc.tensor.matmul(G7, lhsT=wT[:, 1, :], rhs=msgT[:, :], start=False, stop=True)
            nc.tensor.matmul(G5, lhsT=wT[:, 2, :], rhs=msgT[:, :], start=False, stop=True).then_inc(s_rzps, 1)
            nc.tensor.matmul(ps[:, 3, :], lhsT=wT[:, 6, :], rhs=hT[:, :], start=True, stop=True)
            nc.tensor.matmul(ps[:, 2, :], lhsT=wT[:, 3, :], rhs=msgT[:, :], start=True, stop=True).then_inc(s_nps, 1)
            pe.wait_ge(s_qkl, NC - 2)
            normalised(NC - 2, G6)

            def logits(c, n):
                pc, j, odd = tile_of(n)
                U = NK * c + n
                if not odd and j == 0:
                    pe.wait_ge(s_mk, NGRP * c + pc // 2 + 1)
                if not (isinstance(c, int) and U < NB):
                    pe.wait_ge(s_pl, U - NB + 1)
                bank = ps[:, n % NB, :]
                if not odd:
                    for r in range(R):
                        block_T(bank[:, r * P:(r + 1) * P], tile_cols(masks[:, pc // 2 % 2, r, :], j), first=(r == 0))
                qc = bass.ds(c * CH, CH)
                for kk, qq in ((k_hi, q_hi), (k_hi, q_lo), (k_lo, q_hi)):
                    last = nc.tensor.matmul(bank, lhsT=tile_cols(kk[:, pc * PIECE:(pc + 1) * PIECE], j), rhs=qq[:, qc],
                                            start=(odd and qq is q_hi and kk is k_hi), stop=(kk is k_lo),
                                            skip_group_check=True)
                last.then_inc(s_s, 1)

            def weigh(c, n):
                pc, j, _ = tile_of(n)
                pe.wait_ge(s_pl, NK * c + n + 1)
                for r in range(R):
                    if n == 0 and not (isinstance(c, int) and c == 0):
                        pe.wait_ge(s_accd if r < 2 else s_acca, 2 * c - 1 + r % 2)
                    hi = (tile_cols(p_hi[:, n % NB, :], r), 0)
                    lo = (tile_cols(p_lo[:, n % NB, :], r), D)
                    for i, (weights, col) in enumerate((hi, lo) if n == 0 else (lo, hi)):
                        last = nc.tensor.matmul(accs[r][:, col:W], lhsT=weights, rhs=vals[:, KB * pc + j, col:W],
                                                start=(n == 0 and i == 0), stop=(n == NK - 1 and i == 1),
                                                skip_group_check=True)
                last.then_inc(s_pv, 1)

            def chunk1(c, final):
                for n in range(NK):
                    if n + AHEAD < NK:
                        logits(c, n + AHEAD)
                    elif not final:
                        logits(c + 1, n + AHEAD - NK)
                    weigh(c, n)

            gru(NC - 1, GATE_T)
            for n in range(AHEAD):
                logits(0, n)
            pe.wait_ge(s_qkl, NC - 1)
            pe.wait_ge(s_x1, NC)
            pe.wait_ge(s_vl, NC - 1)
            pe.wait_ge(s_ones, 1)
            for n in range(5):
                logits(0, n + AHEAD)
                weigh(0, n)
            normalised(NC - 1, ps[:, 0, :])
            weigh(0, 5)
            weigh(0, 6)
            pe.wait_ge(s_qkl, NC)
            logits(0, 8)
            logits(0, 9)
            weigh(0, 7)
            logits(0, 10)
            for n in range(8, NK):
                if n == 25:
                    pe.wait_ge(s_vl, NC)
                logits(*((0, n + AHEAD) if n + AHEAD < NK else (1, n + AHEAD - NK)))
                weigh(0, n)
            with pe.Fori(1, NC - 1) as c:
                chunk1(c, False)
            chunk1(NC - 1, True)

            def general(c):
                pe.wait_ge(s_gdiag, c + 1)
                for r in range(R):
                    last = nc.tensor.matmul(tile_cols(ps[:, 2, :], r), lhsT=rT[:, 0:P], rhs=hT[:, r * P:(r + 1) * P],
                                            start=True, stop=True, skip_group_check=True)
                last.then_inc(s_gbc, 1)
                for n in range(NK):
                    pc, j = n // KB, n % KB
                    if j == 0:
                        pe.wait_ge(s_gmk, NP * c + pc + 1)
                    for r in range(R):
                        block_T(ps[:, 0, r * P:(r + 1) * P], tile_cols(masks[:, 0, r, :], j))
                    qc = bass.ds(c * CH, CH)
                    for kk, qq in ((k_hi, q_hi), (k_hi, q_lo), (k_lo, q_hi)):
                        last = nc.tensor.matmul(ps[:, 1, :], lhsT=tile_cols(kk[:, pc * PIECE:(pc + 1) * PIECE], j),
                                                rhs=qq[:, qc], start=(qq is q_hi and kk is k_hi), stop=(kk is k_lo))
                    last.then_inc(s_gs, 1)
                    pe.wait_ge(s_gpl, NK * c + n + 1)
                    if n == 0:
                        pe.wait_ge(s_gacc, c + 1)
                    for r in range(R):
                        hi = (tile_cols(p_hi[:, 0, :], r), 0)
                        lo = (tile_cols(p_lo[:, 0, :], r), D)
                        for i, (weights, col) in enumerate((hi, lo) if n == 0 else (lo, hi)):
                            last = nc.tensor.matmul(accs[r][:, col:W], lhsT=weights, rhs=vals[:, n, col:W],
                                                    start=(n == 0 and i == 0), stop=(n == NK - 1 and i == 1),
                                                    skip_group_check=True)
                    last.then_inc(s_gpv, 1)

            pe.wait_ge(s_flag, 1)
            with pe.If(pe.value_load(flag[0:1, 0:1], min_val=0, max_val=1) > 0):
                pe.wait_ge(s_acca, 2 * NC)
                pe.wait_ge(s_accd, 2 * NC)
                with pe.Fori(0, NC) as c:
                    general(c)


_INS = ["x", "adj", "L0_gnn_W_msg", "L0_gnn_b_msg", "L0_gnn_W_ih", "L0_gnn_W_hh", "L0_gnn_b_ih", "L0_gnn_b_hh",
        "L1_gnn_beta"]
_OUTS = [((4096, 128), "float32")]


def kernel(**inputs):
    import numpy as _np
    import concourse.bacc as _bacc
    from concourse import mybir as _mybir
    from concourse.bass_utils import run_bass_kernel_spmd as _run

    nc = _bacc.Bacc("TRN2", target_bir_lowering=False, num_devices=1)
    arrays, args = {}, []
    for name in _INS:
        a = _np.ascontiguousarray(inputs[name])
        arrays[f"in_{name}_dram"] = a
        args.append(nc.dram_tensor(f"in_{name}_dram", a.shape, _mybir.dt.from_np(a.dtype), kind="ExternalInput").ap())
    for i, (shape, dtype) in enumerate(_OUTS):
        dt = _mybir.dt.from_np(_np.dtype(dtype))
        args.append(nc.dram_tensor(f"out_{i}_dram", shape, dt, kind="ExternalOutput").ap())
    gnn_gru_then_masked_attention(nc, *args)
    r = _run(nc, [arrays], core_ids=[0])
    return r.results[0]["out_0_dram"]
```
